# Optimizing a Trainium2 kernel written in Bass

```python
import numpy as np
import jax
import jax.numpy as jnp

def _softmax(x, axis=-1):
    return jax.nn.softmax(x, axis=axis)

def _gelu(x):
    return jax.nn.gelu(x, approximate=True)

def _silu(x):
    return jax.nn.silu(x)

def _sigmoid(x):
    return jax.nn.sigmoid(x)

def _layernorm(x, axis=-1, eps=1e-05):
    m = jnp.mean(x, axis=axis, keepdims=True)
    v = jnp.var(x, axis=axis, keepdims=True)
    return (x - m) / jnp.sqrt(v + eps)

def _scatter_add(tgt, idx, src, axis=0):
    return tgt.at[idx].add(src)

def _segment_sum(src, seg, n):
    return jax.ops.segment_sum(src, seg, n)
kernel_name = 'mk_gnn_resnorm_d4_gnn_r8_a0bdeb'

def setup_inputs(seed: int=0):
    np.random.seed(seed)
    _w = jnp.asarray

    def _rec_inputs():
        import jax
        import jax.numpy as jnp
        _gk = jax.random.key(seed)
        x = -0.000202 + 1 * jax.random.normal(jax.random.fold_in(_gk, 1), (12500, 64), jnp.float32)
        src = jax.random.randint(jax.random.fold_in(_gk, 2), (400000,), 0, 12500, jnp.int32)
        dst = jax.random.randint(jax.random.fold_in(_gk, 3), (400000,), 0, 12500, jnp.int32)
        _o = jnp.argsort(dst, stable=True)
        src = src[_o]
        dst = dst[_o]
        edge_attr_64 = jax.random.uniform(jax.random.fold_in(_gk, 12), (400000, 64), jnp.float32, 0.0, 1)
        edge_weight = jax.random.uniform(jax.random.fold_in(_gk, 14), (400000,), jnp.float32, 0.0, 0.999998)
        return (x, src, dst, edge_attr_64, edge_weight)
    x, src, dst, edge_attr_64, edge_weight = _rec_inputs()

    def _L0_gnn_setup():
        import jax, jax.numpy as jnp
        import numpy as np
        N_NODES = 12500
        N_EDGES = 200000
        N_IN = 64
        N_OUT = 64
        key = jax.random.key(seed)
        k_x, k_w, k_src, k_dst, k_val = jax.random.split(key, 5)
        X = jax.random.normal(k_x, (N_NODES, N_IN), dtype=jnp.float32)
        limit = float(np.sqrt(6.0 / (N_IN + N_OUT)))
        W = jax.random.uniform(k_w, (N_IN, N_OUT), dtype=jnp.float32, minval=-limit, maxval=limit)
        edge_src = jax.random.randint(k_src, (N_EDGES,), 0, N_NODES, dtype=jnp.int32)
        edge_dst = jax.random.randint(k_dst, (N_EDGES,), 0, N_NODES, dtype=jnp.int32)
        edge_val = jax.random.uniform(k_val, (N_EDGES,), dtype=jnp.float32)
        return {'X': X, 'W': W, 'edge_val': edge_val, 'edge_src': edge_src, 'edge_dst': edge_dst}
    _L0_gnn_all = _L0_gnn_setup()
    _L0_gnn_in = {k: v for k, v in _L0_gnn_all.items() if k in ('W',)}
    del _L0_gnn_all

    def _L1_gnn_setup():
        import jax, jax.numpy as jnp
        import numpy as np
        N, E, D, K = (12500, 156250, 64, 64)
        key = jax.random.key(seed)
        ks = jax.random.split(key, 12)
        s = 1.0 / np.sqrt(D)
        return {'x': jax.random.normal(ks[0], (N, D), dtype=jnp.float32), 'i': jax.random.randint(ks[1], (E,), 0, N), 'j': jax.random.randint(ks[2], (E,), 0, N), 'rbf': jax.random.uniform(ks[3], (E, K), dtype=jnp.float32), 'Wf1': jax.random.uniform(ks[4], (D, K), jnp.float32, -s, s), 'bf1': jax.random.uniform(ks[5], (D,), jnp.float32, -s, s), 'Wf2': jax.random.uniform(ks[6], (D, D), jnp.float32, -s, s), 'bf2': jax.random.uniform(ks[7], (D,), jnp.float32, -s, s), 'Wl': jax.random.uniform(ks[8], (D, D), jnp.float32, -s, s), 'bl': jax.random.uniform(ks[9], (D,), jnp.float32, -s, s), 'gamma': jnp.ones((D,), jnp.float32), 'beta': jnp.zeros((D,), jnp.float32)}
    _L1_gnn_all = _L1_gnn_setup()
    _L1_gnn_in = {k: v for k, v in _L1_gnn_all.items() if k in ('Wf1', 'bf1', 'Wf2', 'bf2', 'Wl', 'bl', 'gamma', 'beta')}
    del _L1_gnn_all

    def _L2_gnn_setup():
        import jax, jax.numpy as jnp
        import numpy as np
        N_NODES = 12500
        N_EDGES = 125000
        D_IN = 64
        D_OUT = 64
        key = jax.random.key(seed)
        k1, k2, k3, k4, k5 = jax.random.split(key, 5)
        x = jax.random.normal(k1, (N_NODES, D_IN), dtype=jnp.float32)
        edge_index = jax.random.randint(k2, (2, N_EDGES), 0, N_NODES, dtype=jnp.int64)
        bound1 = float(np.sqrt(6.0 / D_IN)) * np.sqrt(2.0)
        bound2 = float(np.sqrt(6.0 / D_OUT)) * np.sqrt(2.0)
        W1 = jax.random.uniform(k3, (D_IN, D_OUT), minval=-bound1, maxval=bound1, dtype=jnp.float32)
        b1 = jnp.zeros((D_OUT,), dtype=jnp.float32)
        W2 = jax.random.uniform(k4, (D_OUT, D_OUT), minval=-bound2, maxval=bound2, dtype=jnp.float32)
        b2 = jnp.zeros((D_OUT,), dtype=jnp.float32)
        return {'x': x, 'edge_index': edge_index, 'W1': W1, 'b1': b1, 'W2': W2, 'b2': b2}
    _L2_gnn_all = _L2_gnn_setup()
    _L2_gnn_in = {k: v for k, v in _L2_gnn_all.items() if k in ('W1', 'b1', 'W2', 'b2')}
    del _L2_gnn_all

    def _L3_gnn_setup():
        import jax, jax.numpy as jnp
        import numpy as np
        N = 6250
        E = 100000
        DIN = 64
        DOUT = 64
        key = jax.random.key(seed)
        k1, k2, k3 = jax.random.split(key, 3)
        x = jax.random.normal(k1, (N, DIN), dtype=jnp.float32)
        edge_index = jax.random.randint(k2, (2, E), 0, N, dtype=jnp.int32)
        limit = float(np.sqrt(6.0 / (DIN + DOUT)))
        weight = jax.random.uniform(k3, (DIN, DOUT), dtype=jnp.float32, minval=-limit, maxval=limit)
        bias = jnp.zeros((DOUT,), dtype=jnp.float32)
        return {'x': x, 'edge_index': edge_index, 'weight': weight, 'bias': bias}
    _L3_gnn_all = _L3_gnn_setup()
    _L3_gnn_in = {k: v for k, v in _L3_gnn_all.items() if k in ('weight', 'bias')}
    del _L3_gnn_all
    return {'x': x, 'src': src, 'dst': dst, 'edge_attr_64': edge_attr_64, 'edge_weight': edge_weight, 'L0_gnn_W': _L0_gnn_in['W'], 'L1_gnn_Wf1': _L1_gnn_in['Wf1'], 'L1_gnn_bf1': _L1_gnn_in['bf1'], 'L1_gnn_Wf2': _L1_gnn_in['Wf2'], 'L1_gnn_bf2': _L1_gnn_in['bf2'], 'L1_gnn_Wl': _L1_gnn_in['Wl'], 'L1_gnn_bl': _L1_gnn_in['bl'], 'L1_gnn_gamma': _L1_gnn_in['gamma'], 'L1_gnn_beta': _L1_gnn_in['beta'], 'L2_gnn_W1': _L2_gnn_in['W1'], 'L2_gnn_b1': _L2_gnn_in['b1'], 'L2_gnn_W2': _L2_gnn_in['W2'], 'L2_gnn_b2': _L2_gnn_in['b2'], 'L3_gnn_weight': _L3_gnn_in['weight'], 'L3_gnn_bias': _L3_gnn_in['bias']}

def reference(x, src, dst, edge_attr_64, edge_weight, L0_gnn_W, L1_gnn_Wf1, L1_gnn_bf1, L1_gnn_Wf2, L1_gnn_bf2, L1_gnn_Wl, L1_gnn_bl, L1_gnn_gamma, L1_gnn_beta, L2_gnn_W1, L2_gnn_b1, L2_gnn_W2, L2_gnn_b2, L3_gnn_weight, L3_gnn_bias):
    import jax
    import jax.numpy as jnp

    def _L0_gnn_ref(X, W, edge_val, edge_src, edge_dst):
        import jax, jax.numpy as jnp
        import numpy as np
        N_NODES = 12500
        N_EDGES = 200000
        N_IN = 64
        N_OUT = 64
        h = X @ W
        msgs = h[edge_src] * edge_val[:, None]
        agg = jax.ops.segment_sum(msgs, edge_dst, num_segments=N_NODES)
        return jax.nn.relu(agg)

    def _L1_gnn_ref(x, i, j, rbf, Wf1, bf1, Wf2, bf2, Wl, bl, gamma, beta):
        import jax, jax.numpy as jnp
        import numpy as np
        N, E, D, K = (12500, 156250, 64, 64)
        Wxh = x @ Wl.T + bl
        h = jax.nn.silu(rbf @ Wf1.T + bf1)
        f_ij = h @ Wf2.T + bf2
        msg = f_ij * Wxh[j]
        agg = jax.ops.segment_sum(msg, i, num_segments=x.shape[0])
        y = x + agg
        mu = jnp.mean(y, axis=-1, keepdims=True)
        var = jnp.var(y, axis=-1, keepdims=True)
        return (y - mu) * jax.lax.rsqrt(var + 1e-05) * gamma + beta

    def _L2_gnn_ref(x, edge_index, W1, b1, W2, b2):
        import jax, jax.numpy as jnp
        import numpy as np
        N_NODES = 12500
        N_EDGES = 125000
        D_IN = 64
        D_OUT = 64
        src = edge_index[0]
        dst = edge_index[1]
        msgs = x[src]
        agg = jax.ops.segment_sum(msgs, dst, num_segments=N_NODES)
        h = x + agg
        h = jax.nn.relu(h @ W1 + b1)
        return h @ W2 + b2

    def _L3_gnn_ref(x, edge_index, weight, bias):
        import jax, jax.numpy as jnp
        import numpy as np
        N = 6250
        E = 100000
        DIN = 64
        DOUT = 64
        n = x.shape[0]
        row, col = (edge_index[0], edge_index[1])
        deg = jax.ops.segment_sum(jnp.ones_like(row, dtype=x.dtype), row, num_segments=n)
        dinv = jnp.where(deg > 0, jax.lax.rsqrt(deg), jnp.zeros_like(deg))
        xw = x @ weight
        msgs = (dinv[row] * dinv[col])[:, None] * xw[col]
        agg = jax.ops.segment_sum(msgs, row, num_segments=n)
        return agg + bias
    edge_index = jnp.stack([src, dst])
    x = _layernorm(x + _L0_gnn_ref(x, L0_gnn_W, edge_weight, src, dst), axis=-1)
    x = _layernorm(x + _L1_gnn_ref(x, src, dst, edge_attr_64, L1_gnn_Wf1, L1_gnn_bf1, L1_gnn_Wf2, L1_gnn_bf2, L1_gnn_Wl, L1_gnn_bl, L1_gnn_gamma, L1_gnn_beta), axis=-1)
    x = _layernorm(x + _L2_gnn_ref(x, edge_index, L2_gnn_W1, L2_gnn_b1, L2_gnn_W2, L2_gnn_b2), axis=-1)
    x = _layernorm(x + _L3_gnn_ref(x, edge_index, L3_gnn_weight, L3_gnn_bias), axis=-1)
    return x

_drawn_inputs = setup_inputs


def setup_inputs(seed=0):
    import zlib

    import numpy as np

    out = dict(_drawn_inputs(seed))
    spreads = {'L1_gnn_gamma': (1.0, 0.2),
     'L1_gnn_beta': (0.0, 0.1),
     'L2_gnn_b1': (0.0, 0.8),
     'L2_gnn_b2': (0.0, 0.8),
     'L3_gnn_bias': (0.0, 0.1)}
    factors = {}
    for name, (base, spread) in spreads.items():
        noise = np.random.default_rng([zlib.crc32(name.encode()), seed]).standard_normal(out[name].shape)
        drawn = base * np.exp(spread * noise) if base else spread * noise
        out[name] = jnp.asarray(drawn.astype(out[name].dtype))
    for name, factor in factors.items():
        out[name] = (out[name] * factor).astype(out[name].dtype)
    return out
```

```python
import numpy as np
import concourse.bass as bass
from concourse import mybir
from contextlib import ExitStack

F32 = mybir.dt.float32
I32 = mybir.dt.int32
ALU = mybir.AluOpType
ACT = mybir.ActivationFunctionType
AX = mybir.AxisListType

NODES, EDGES, D = 12500, 400000, 64
P = 128
TILES = EDGES // P
GROUP = 25
TURNS = TILES // GROUP
CHUNK = 5
CHUNKS = GROUP // CHUNK
TABLES = CHUNK
AHEAD = 10
HALVES = ((0, 10), (10, 25))
NP_ = 125
NT = NODES // NP_
ROWS = 12800
ZR = ROWS // P // CHUNK
CREDIT = 5
NCH = 20
QUAD = 4
EPS = 1e-5


class Counter:

    def __init__(self, sem):
        self.sem, self.base = sem, 0

    def at(self, n):
        return n + self.base


def build(nc, a, out):
    ctx = ExitStack()
    with ctx:
        def sb(name, shape, dt=F32):
            return ctx.enter_context(nc.sbuf_tensor(name, shape, dt))

        def ps(name):
            return ctx.enter_context(nc.psum_tensor(name, [P, 512], F32))

        def counter(name):
            return Counter(ctx.enter_context(nc.semaphore(name)))

        table = [nc.dram_tensor(f"node_table_{n}", (NODES, D), F32, kind="Internal").ap() for n in range(4)]
        width = [D, D + 1, D, D]
        part = [[nc.dram_tensor(f"partial_{n}_{k}", (ROWS, width[n]), F32, kind="Internal").ap()
                 for k in range(TABLES)] for n in range(4)]

        ident = sb("ident", [P, P])
        upper = sb("upper", [P, P])
        trash = sb("trash", [P, 1])
        zeros = sb("zeros", [P, ZR * (D + 1)])
        w0 = sb("w0", [D, D])
        wl = sb("wl", [D + 1, D])
        wf1 = sb("wf1", [D, D])
        bf1 = sb("bf1", [D, 1])
        wf2 = sb("wf2", [D + 1, D])
        w1 = sb("w1", [D, D])
        b1 = sb("b1", [D, 1])
        w2 = sb("w2", [D + 1, D])
        w3 = sb("w3", [D, D])
        gamma = sb("gamma", [NP_, D])
        beta = sb("beta", [NP_, D])
        bias3 = sb("bias3", [NP_, D])

        xr = sb("x_rows", [NP_, NT * D])
        dinv = sb("dinv", [NP_, NT])

        psb = [ps(f"ps_{n}") for n in range(8)]

        settled = ctx.enter_context(nc.semaphore("settled"))
        s_const = counter("s_const")
        s_load = counter("s_load")

        def settle(eng):
            eng.sem_inc(settled, 1)

        loads = [(w0[:, :], a["L0_gnn_W"]), (wl[0:D, :], a["WlT"]), (wl[D:D + 1, :], a["bl"]),
                 (wf1[:, :], a["Wf1T"]), (bf1[:, :], a["bf1"]), (wf2[0:D, :], a["Wf2T"]), (wf2[D:D + 1, :], a["bf2"]),
                 (w1[:, :], a["L2_gnn_W1"]), (b1[:, :], a["b1"]), (w2[0:D, :], a["L2_gnn_W2"]), (w2[D:D + 1, :], a["b2"]),
                 (w3[:, :], a["L3_gnn_weight"]),
                 (gamma[:, :], a["gamma"].to_broadcast([NP_, D])), (beta[:, :], a["beta"].to_broadcast([NP_, D])),
                 (bias3[:, :], a["bias3"].to_broadcast([NP_, D])),
                 (xr[:, :], a["x"].rearrange("(p t) d -> p (t d)", p=NP_))]

        with nc.Block() as block:
            @block.sync
            def _(sp):
                for dst, src in loads:
                    sp.dma_start(dst, src).then_inc(s_load.sem, 16)
                sp.wait_ge(s_load.sem, 16 * len(loads))

            @block.gpsimd
            def _(pool):
                pool.memset(ident[:, :], 0.0).then_inc(s_const.sem, 1)
                pool.memset(upper[:, :], 1.0).then_inc(s_const.sem, 1)
                pool.memset(zeros[:, :], 0.0).then_inc(s_const.sem, 1)
                pool.iota(trash[:, :], pattern=[[0, 1]], base=NODES, channel_multiplier=1,
                          allow_small_or_imprecise_dtypes=True).then_inc(s_const.sem, 1)
                pool.wait_ge(s_const.sem, 4)
                pool.affine_select(out=ident[:, :], in_=ident[:, :], compare_op=ALU.not_equal, fill=1.0,
                                   base=0, pattern=[[-1, P]], channel_multiplier=1).then_inc(s_const.sem, 1)
                pool.affine_select(out=upper[:, :], in_=upper[:, :], compare_op=ALU.is_ge, fill=0.0,
                                   base=0, pattern=[[1, P]], channel_multiplier=-1).then_inc(s_const.sem, 1)
                pool.wait_ge(s_const.sem, 6)

        sem_gidx = [counter(f"gidx_in_{h}") for h in range(2)]
        sem_sidx = [counter(f"sidx_in_{h}") for h in range(2)]
        sem_ew = [counter(f"ew_in_{h}") for h in range(2)]
        sem_ea = [counter(f"ea_in_{h}") for h in range(2)]
        sem_gath = [counter(f"gathered_{j}") for j in range(GROUP)]
        sem_tab = [counter(f"added_{k}") for k in range(TABLES)]
        s_idxf = counter("idxf_done")
        s_bc = counter("bcast_done")
        s_sel = counter("sel_done")
        s_tr = counter("trash_done")
        s_fin = counter("fin_done")
        s_msg = counter("msg_done")
        s_f1 = counter("f1_done")
        s_h = counter("silu_done")
        s_f2 = counter("f2_done")
        s_mg = counter("merge_done")
        s_out = counter("out_done")

        def edge_pass(n, gidx_d, sidx_d, ew_d=None, ea_d=None):
            W = width[n]
            made = ew_d is not None or ea_d is not None
            ectx = ExitStack()
            with ectx:
                def sbe(name, shape, dt=F32):
                    return ectx.enter_context(nc.sbuf_tensor(f"{name}_{n}", shape, dt))

                gidx = sbe("gidx", [P, GROUP], I32)
                sidx = sbe("sidx", [P, GROUP], I32)
                idxf = sbe("idxf", [P, GROUP])
                cnt = sbe("cnt", [P, GROUP])
                off = sbe("off", [P, GROUP])
                fin = sbe("fin", [P, GROUP], I32)
                ew = sbe("ew", [P, GROUP])
                g = sbe("g", [P, GROUP, D])
                msg = sbe("msg", [P, GROUP, W]) if made else g
                sel = sbe("sel", [P, GROUP, P])
                o = sbe("o", [P, GROUP, W])
                ea = sbe("ea", [D, GROUP * P]) if ea_d is not None else None
                hT = sbe("hT", [D + 1, CHUNK * P]) if ea_d is not None else None

                def bc(k):
                    return psb[k // 4][:, (k % 4) * P:(k % 4 + 1) * P]

                HC = CHUNK * P // 2
                merged = psb[2][:, 0:CHUNK * W]
                f2 = psb[3][:, 0:CHUNK * D]
                f1 = [psb[4][0:D, 0:HC], psb[5][0:D, 0:HC]]

                def load_half(sp, h, r):
                    lo, hi = HALVES[h]

                    def cols(src):
                        return src[:, bass.ds(r * GROUP + lo, hi - lo)]
                    sp.dma_start(gidx[:, lo:hi], cols(gidx_d)).then_inc(sem_gidx[h].sem, 16)
                    sp.dma_start(sidx[:, lo:hi], cols(sidx_d)).then_inc(sem_sidx[h].sem, 16)
                    if ew_d is not None:
                        sp.dma_start(ew[:, lo:hi], cols(ew_d)).then_inc(sem_ew[h].sem, 16)
                    if ea_d is not None:
                        sp.dma_start(ea[:, lo * P:hi * P], ea_d[:, bass.ds(r * (GROUP * P) + lo * P, (hi - lo) * P)])\
                            .then_inc(sem_ea[h].sem, 16)

                def half_of(c):
                    return 0 if c * CHUNK < HALVES[0][1] else 1

                def tables_free(eng, r, c):
                    for k in range(TABLES):
                        eng.wait_ge(sem_tab[k].sem, sem_tab[k].at(16 * (CREDIT * r + c + 1)) if isinstance(r, int)
                                    else r * (16 * CREDIT) + sem_tab[k].at(16 * (c + 1)))

                def wait(eng, cnt_, r, n_, per=CHUNKS, credit=CREDIT):
                    eng.wait_ge(cnt_.sem, r * per + (cnt_.at(credit + n_)))

                with nc.Block() as block:
                    @block.sync
                    def _(sp):
                        for h in range(2):
                            load_half(sp, h, 0)

                        def body(r):
                            for h in range(2):
                                wait(sp, s_mg, r, HALVES[h][1] // CHUNK)
                                settle(sp)
                                load_half(sp, h, r + 1)
                        with sp.Fori(0, TURNS - 1) as r:
                            body(r)

                    @block.gpsimd
                    def _(pool):
                        def gather(j, r):
                            c = j // CHUNK
                            h = half_of(c)
                            if j % CHUNK == 0:
                                pool.wait_ge(sem_gidx[h].sem, r * 16 + sem_gidx[h].at(16))
                                wait(pool, s_mg, r, c + 1 - CHUNKS)
                                settle(pool)
                            pool.indirect_dma_start(
                                out=g[:, j, :], out_offset=None, in_=table[n],
                                in_offset=bass.IndirectOffsetOnAxis(ap=gidx[:, j:j + 1], axis=0))\
                                .then_inc(sem_gath[j].sem, 16)

                        def scatter(j, r):
                            c, k = divmod(j, CHUNK)
                            if k == 0:
                                wait(pool, s_out, r, c + 1)
                                wait(pool, s_fin, r, c + 1)
                            pool.wait_ge(sem_tab[k].sem, r * (16 * CHUNKS) + sem_tab[k].at(16 * (CREDIT + c)))
                            settle(pool)
                            pool.indirect_dma_start(
                                out=part[n][k], out_offset=bass.IndirectOffsetOnAxis(ap=fin[:, j:j + 1], axis=0),
                                in_=o[:, j, :], in_offset=None, compute_op=ALU.add)\
                                .then_inc(sem_tab[k].sem, 16)

                        for q in range(CREDIT):
                            for k in range(TABLES):
                                if q:
                                    pool.wait_ge(sem_tab[k].sem, sem_tab[k].at(16 * q))
                                dst = part[n][k].rearrange("(p a) w -> p (a w)", p=P)
                                pool.dma_start(dst[:, q * ZR * W:(q + 1) * ZR * W], zeros[:, 0:ZR * W])\
                                    .then_inc(sem_tab[k].sem, 16)
                        for h in range(2):
                            pool.wait_ge(sem_gidx[h].sem, sem_gidx[h].at(16))
                        for j in range(AHEAD):
                            pool.indirect_dma_start(
                                out=g[:, j, :], out_offset=None, in_=table[n],
                                in_offset=bass.IndirectOffsetOnAxis(ap=gidx[:, j:j + 1], axis=0))\
                                .then_inc(sem_gath[j].sem, 16)

                        def body(r, last):
                            for j in range(GROUP):
                                ahead = j + AHEAD
                                if ahead < GROUP:
                                    gather(ahead, r)
                                elif not last:
                                    gather(ahead - GROUP, r + 1)
                                scatter(j, r)
                        with pool.Fori(0, TURNS - 1) as r:
                            body(r, False)
                        body(TURNS - 1, True)
                        settle(pool)
                        for k in range(TABLES):
                            pool.wait_ge(sem_tab[k].sem, sem_tab[k].at(16 * CHUNKS * (TURNS + 1)))

                    @block.vector
                    def _(dve):
                        for s in (s_idxf, s_sel, s_tr, s_fin, s_msg):
                            dve.sem_inc(s.sem, CREDIT)
                        if ea_d is not None:
                            dve.memset(msg[:, :, D:D + 1], 1.0).then_inc(s_h.sem, 1)

                        def body(r):
                            for c in range(CHUNKS):
                                lo, hi = c * CHUNK, (c + 1) * CHUNK
                                h = half_of(c)
                                if lo == HALVES[h][0]:
                                    dve.wait_ge(sem_sidx[h].sem, r * 16 + sem_sidx[h].at(16))
                                    wait(dve, s_mg, r, HALVES[h][1] // CHUNK - CHUNKS)
                                    wait(dve, s_fin, r, HALVES[h][1] // CHUNK - CHUNKS)
                                    settle(dve)
                                    dve.tensor_copy(idxf[:, HALVES[h][0]:HALVES[h][1]], sidx[:, HALVES[h][0]:HALVES[h][1]])\
                                        .then_inc(s_idxf.sem, 1)
                                    dve.wait_ge(s_idxf.sem, r * 2 + s_idxf.at(CREDIT + h + 1))
                                wait(dve, s_bc, r, c + 1)
                                wait(dve, s_mg, r, c + 1 - CHUNKS)
                                wait(dve, s_tr, r, c + 1 - CHUNKS)
                                settle(dve)
                                for j in range(lo, hi):
                                    i = dve.scalar_tensor_tensor(
                                        out=sel[:, j, :], in0=bc(j - lo), scalar=idxf[:, j:j + 1], in1=upper[:, :],
                                        op0=ALU.is_equal, op1=ALU.mult, accum_out=cnt[:, j:j + 1])
                                i.then_inc(s_sel.sem, 1)
                                wait(dve, s_sel, r, c + 1)
                                wait(dve, s_fin, r, c + 1 - CHUNKS)
                                settle(dve)
                                dve.tensor_scalar(off[:, lo:hi], cnt[:, lo:hi], 1.5, trash[:, 0:1], ALU.is_gt, ALU.mult)\
                                    .then_inc(s_tr.sem, 1)
                                wait(dve, s_tr, r, c + 1)
                                tables_free(dve, r, c)
                                settle(dve)
                                dve.tensor_tensor(fin[:, lo:hi], off[:, lo:hi], idxf[:, lo:hi], ALU.max)\
                                    .then_inc(s_fin.sem, 1)
                                if not made:
                                    continue
                                for j in range(lo, hi):
                                    dve.wait_ge(sem_gath[j].sem, r * 16 + sem_gath[j].at(16))
                                if ew_d is not None:
                                    dve.wait_ge(sem_ew[h].sem, r * 16 + sem_ew[h].at(16))
                                    wait(dve, s_mg, r, c + 1 - CHUNKS)
                                    settle(dve)
                                    dve.tensor_tensor(msg[:, lo:hi, :], g[:, lo:hi, :],
                                                      ew[:, lo:hi].unsqueeze(2).to_broadcast([P, CHUNK, D]), ALU.mult)\
                                        .then_inc(s_msg.sem, 1)
                                else:
                                    wait(dve, s_f2, r, c + 1)
                                    settle(dve)
                                    dve.tensor_tensor(msg[:, lo:hi, 0:D], g[:, lo:hi, :],
                                                      f2.rearrange("p (k d) -> p k d", d=D), ALU.mult)\
                                        .then_inc(s_msg.sem, 1)
                        with dve.Fori(0, TURNS) as r:
                            body(r)

                    @block.tensor
                    def _(pe):
                        for s in (s_bc, s_f1, s_f2, s_mg):
                            pe.sem_inc(s.sem, CREDIT)

                        def body(r):
                            for c in range(CHUNKS):
                                lo, hi = c * CHUNK, (c + 1) * CHUNK
                                h = half_of(c)
                                if lo == HALVES[h][0]:
                                    pe.wait_ge(s_idxf.sem, r * 2 + s_idxf.at(CREDIT + h + 1))
                                wait(pe, s_sel, r, c)
                                settle(pe)
                                for j in range(lo, hi):
                                    i = pe.matmul(bc(j - lo), idxf[:, j:j + 1].to_broadcast([P, P]), ident[:, :],
                                                  start=True, stop=True)
                                i.then_inc(s_bc.sem, 1)
                                if ea_d is not None:
                                    pe.wait_ge(sem_ea[h].sem, r * 16 + sem_ea[h].at(16))
                                    wait(pe, s_h, r, c)
                                    settle(pe)
                                    for b in range(2):
                                        i = pe.matmul(f1[b], wf1[:, :], ea[:, lo * P + b * HC:lo * P + (b + 1) * HC],
                                                      start=True, stop=True)
                                    i.then_inc(s_f1.sem, 1)
                                    wait(pe, s_h, r, c + 1)
                                    wait(pe, s_msg, r, c)
                                    settle(pe)
                                    for k in range(CHUNK):
                                        i = pe.matmul(f2[:, k * D:(k + 1) * D], hT[:, k * P:(k + 1) * P], wf2[:, :],
                                                      start=True, stop=True)
                                    i.then_inc(s_f2.sem, 1)
                                wait(pe, s_sel, r, c + 1)
                                wait(pe, s_out, r, c)
                                if made:
                                    wait(pe, s_msg, r, c + 1)
                                else:
                                    for j in range(lo, hi):
                                        pe.wait_ge(sem_gath[j].sem, r * 16 + sem_gath[j].at(16))
                                settle(pe)
                                for j in range(lo, hi):
                                    k = j - lo
                                    i = pe.matmul(merged[:, k * W:(k + 1) * W], sel[:, j, :], msg[:, j, :],
                                                  start=True, stop=True)
                                i.then_inc(s_mg.sem, 1)
                        with pe.Fori(0, TURNS) as r:
                            body(r)

                    @block.scalar
                    def _(act):
                        act.sem_inc(s_out.sem, CREDIT)
                        if ea_d is not None:
                            act.activation(hT[D:D + 1, :], zeros[0:1, 0:CHUNK * P], ACT.Copy, bias=1.0).then_inc(s_h.sem, CREDIT - 1)

                        def body(r):
                            for c in range(CHUNKS):
                                lo, hi = c * CHUNK, (c + 1) * CHUNK
                                if ea_d is not None:
                                    wait(act, s_f1, r, c + 1)
                                    wait(act, s_f2, r, c)
                                    settle(act)
                                    for b in range(2):
                                        i = act.activation(hT[0:D, b * HC:(b + 1) * HC], f1[b], ACT.Silu, bias=bf1[:, 0:1])
                                    i.then_inc(s_h.sem, 1)
                                wait(act, s_mg, r, c + 1)
                                tables_free(act, r, c)
                                settle(act)
                                act.activation(o[:, lo:hi, :], merged.rearrange("p (k w) -> p k w", w=W), ACT.Copy)\
                                    .then_inc(s_out.sem, 1)
                        with act.Fori(0, TURNS) as r:
                            body(r)

            for c_ in sem_gidx + sem_sidx + sem_gath:
                c_.base += 16 * TURNS
            if ew_d is not None:
                for c_ in sem_ew:
                    c_.base += 16 * TURNS
            if ea_d is not None:
                for c_ in sem_ea:
                    c_.base += 16 * TURNS
                for c_ in (s_f1, s_h, s_f2):
                    c_.base += CHUNKS * TURNS + CREDIT
            else:
                for c_ in (s_f1, s_f2):
                    c_.base += CREDIT
            for c_ in sem_tab:
                c_.base += 16 * CHUNKS * (TURNS + 1)
            s_idxf.base += 2 * TURNS + CREDIT
            for c_ in (s_sel, s_tr, s_fin, s_bc, s_mg, s_out):
                c_.base += CHUNKS * TURNS + CREDIT
            s_msg.base += (CHUNKS * TURNS if made else 0) + CREDIT

        n_dve = counter("node_dve")
        n_act = counter("node_act")
        n_pe = counter("node_pe")
        n_part = [counter(f"node_part_{k}") for k in range(TABLES)]
        n_store = counter("node_store")

        class Queue:

            def __init__(self, eng, count, start):
                self.eng, self.c, self.n = eng, count, start

            def step(self, i):
                i.then_inc(self.c.sem, 1)
                self.n += 1
                return self.n

        def node_stage(n, last=False):
            ectx = ExitStack()
            with ectx:
                def sbn(name, shape, dt=F32):
                    return ectx.enter_context(nc.sbuf_tensor(f"{name}_n{n}", shape, dt))
                W = width[n - 1] if n else D
                pin = [sbn(f"pin{k}", [NP_, NCH, W]) for k in range(TABLES)] if n else []
                y = sbn("y", [NP_, NCH, D])
                t = sbn("t", [NP_, NCH, D])
                st = sbn("st", [NP_, 6, NCH])
                xT = sbn("xT", [D + 1, QUAD * NP_])
                hT = sbn("hT", [D + 1, QUAD * NP_])
                tab = sbn("tab", [NP_, NT * D])
                xv = xr[:, :].rearrange("p (t d) -> p t d", d=D)
                tabv = tab[:, :].rearrange("p (t d) -> p t d", d=D)
                psT, psH, psO = psb[0], psb[1], psb[2]

                steps = []
                number = {"dve": n_dve.base, "act": n_act.base, "pe": n_pe.base}

                def do(name, waits, make):
                    number[name] += 1
                    steps.append((name, list(waits), make))
                    return (name, number[name])

                def dve(waits, make):
                    return do("dve", waits, make)

                prev = [None]

                def chain(make, extra=()):
                    w = ([prev[0]] if prev[0] else []) + list(extra)
                    prev[0] = dve(w, make)
                    return prev[0]

                def bcast(s, m=NCH):
                    return s.unsqueeze(2).to_broadcast([NP_, m, D])

                def rows(v, m=NCH):
                    return v.unsqueeze(1).to_broadcast([NP_, m, D])

                def norm(src, dst):
                    s0, s1, s2, s3 = (st[:, i, :] for i in range(4))
                    chain(lambda e: e.tensor_reduce(s0, src, AX.X, ALU.add))
                    chain(lambda e: e.tensor_scalar(s1, s0, 1.0 / D, None, ALU.mult))
                    chain(lambda e: e.tensor_tensor(src, src, bcast(s1), ALU.subtract))
                    chain(lambda e: e.tensor_tensor(t[:, :, :], src, src, ALU.mult))
                    chain(lambda e: e.tensor_reduce(s0, t[:, :, :], AX.X, ALU.add))
                    v = chain(lambda e: e.tensor_scalar(s2, s0, 1.0 / D, EPS, ALU.mult, ALU.add))
                    sd = do("act", [v], lambda e: e.activation(s3, s2, ACT.Sqrt))
                    chain(lambda e: e.reciprocal(s1, s3), [sd])
                    chain(lambda e: e.tensor_tensor(dst, src, bcast(s1), ALU.mult))

                def transposed(src_rows, after):
                    for m in range(QUAD):
                        p = do("pe", after, lambda e, m=m: e.transpose(psT[0:D, m * NP_:(m + 1) * NP_], src_rows[:, m, :],
                                                                      ident[0:NP_, 0:NP_]))
                    return do("act", [p], lambda e: e.activation(xT[0:D, :], psT[0:D, 0:QUAD * NP_], ACT.Copy))

                def product(wT, w, after):
                    k = w.shape[0]
                    for m in range(QUAD):
                        p = do("pe", after, lambda e, m=m: e.matmul(psO[0:NP_, m * D:(m + 1) * D], wT[0:k, m * NP_:(m + 1) * NP_],
                                                                    w, start=True, stop=True))
                    return p
                psOv = psO[0:NP_, 0:QUAD * D].rearrange("p (m d) -> p m d", d=D)

                ones = do("act", [], lambda e: e.activation(xT[D:D + 1, :], zeros[0:1, 0:QUAD * NP_], ACT.Copy, bias=1.0))
                ones = do("act", [], lambda e: e.activation(hT[D:D + 1, :], zeros[0:1, 0:QUAD * NP_], ACT.Copy, bias=1.0))
                part_read = []
                for q in range(NT // NCH if n else 0):
                    xq = xv[:, q * NCH:(q + 1) * NCH, :]
                    chain(lambda e: e.tensor_tensor(pin[0][:, :, :], pin[0][:, :, :], pin[1][:, :, :], ALU.add),
                          [("part", 0, q), ("part", 1, q)])
                    for k in range(2, TABLES):
                        chain(lambda e, k=k: e.tensor_tensor(pin[0][:, :, :], pin[0][:, :, :], pin[k][:, :, :], ALU.add),
                              [("part", k, q)])
                    agg = pin[0][:, :, 0:D]
                    if n == 1:
                        part_read.append(chain(lambda e, xq=xq: e.scalar_tensor_tensor(
                            out=y[:, :, :], in0=agg, scalar=0.0, in1=xq, op0=ALU.max, op1=ALU.add)))
                    elif n == 2:
                        deg, dv = pin[0][:, :, D], dinv[:, q * NCH:(q + 1) * NCH]
                        s4, s5 = st[:, 4, :], st[:, 5, :]
                        c1 = chain(lambda e, deg=deg: e.tensor_scalar(s4, deg, 1.0, None, ALU.max))
                        sd = do("act", [c1], lambda e: e.activation(s5, s4, ACT.Sqrt))
                        chain(lambda e: e.reciprocal(s4, s5), [sd])
                        chain(lambda e, deg=deg: e.tensor_scalar(s5, deg, 0.5, None, ALU.is_gt))
                        chain(lambda e, dv=dv: e.tensor_tensor(dv, s4, s5, ALU.mult))
                        part_read.append(chain(lambda e, xq=xq: e.tensor_tensor(y[:, :, :], agg, xq, ALU.add)))
                        norm(y[:, :, :], y[:, :, :])
                        chain(lambda e: e.tensor_tensor(y[:, :, :], y[:, :, :], rows(gamma[:, :]), ALU.mult))
                        chain(lambda e: e.tensor_tensor(y[:, :, :], y[:, :, :], rows(beta[:, :]), ALU.add))
                        chain(lambda e, xq=xq: e.tensor_tensor(y[:, :, :], y[:, :, :], xq, ALU.add))
                    elif n == 3:
                        part_read.append(chain(lambda e, xq=xq: e.tensor_tensor(y[:, :, :], agg, xq, ALU.add)))
                        for m in range(0, NCH, QUAD):
                            ax = transposed(y[:, m:m + QUAD, :], [prev[0], ones])
                            p = do("pe", [ax], lambda e: e.matmul(psH[0:D, 0:QUAD * NP_], w1[:, :], xT[0:D, :],
                                                                  start=True, stop=True))
                            ah = do("act", [p], lambda e: e.activation(hT[0:D, :], psH[0:D, 0:QUAD * NP_], ACT.Relu,
                                                                       bias=b1[:, 0:1]))
                            p = product(hT, w2[:, :], [ah])
                            chain(lambda e, m=m, xq=xq: e.tensor_tensor(y[:, m:m + QUAD, :], psOv, xq[:, m:m + QUAD, :], ALU.add),
                                  [p])
                    else:
                        dv = dinv[:, q * NCH:(q + 1) * NCH]
                        part_read.append(chain(lambda e, dv=dv: e.tensor_tensor(y[:, :, :], agg, bcast(dv), ALU.mult)))
                        chain(lambda e: e.tensor_tensor(y[:, :, :], y[:, :, :], rows(bias3[:, :]), ALU.add))
                        chain(lambda e, xq=xq: e.tensor_tensor(y[:, :, :], y[:, :, :], xq, ALU.add))
                    norm(y[:, :, :], xq)
                if n in (0, 1, 3):
                    w = {0: w0[:, :], 1: wl[:, :], 3: w3[:, :]}[n]
                    for m in range(0, NT, QUAD):
                        ax = transposed(xv[:, m:m + QUAD, :], [prev[0], ones] if prev[0] else [ones])
                        p = product(xT, w, [ax])
                        dst = tabv[:, m:m + QUAD, :]
                        if n == 3:
                            chain(lambda e, m=m, dst=dst: e.tensor_tensor(dst, psOv, bcast(dinv[:, m:m + QUAD], QUAD), ALU.mult), [p])
                        else:
                            chain(lambda e, dst=dst: e.tensor_copy(dst, psOv), [p])
                final = prev[0]
                src = tab if n in (0, 1, 3) else xr

                counters = {"dve": n_dve, "act": n_act, "pe": n_pe}

                def run(name, eng):
                    for who, waits, make in steps:
                        if who != name:
                            continue
                        for w in waits:
                            if w[0] == "part":
                                eng.wait_ge(n_part[w[1]].sem, n_part[w[1]].at(16 * (w[2] + 1)))
                            else:
                                eng.wait_ge(counters[w[0]].sem, w[1])
                        make(eng).then_inc(counters[name].sem, 1)

                with nc.Block() as block:
                    @block.sync
                    def _(sp):
                        for q in range(NT // NCH if n else 0):
                            if q:
                                sp.wait_ge(n_dve.sem, part_read[q - 1][1])
                            for k in range(TABLES):
                                sp.dma_start(pin[k][:, :, :].rearrange("p a w -> p (a w)"),
                                             part[n - 1][k][0:NODES, :].rearrange("(p a) w -> p (a w)", p=NP_)
                                             [:, q * NCH * W:(q + 1) * NCH * W]).then_inc(n_part[k].sem, 16)
                        sp.wait_ge(n_dve.sem, final[1])
                        dst = out if last else table[n]
                        sp.dma_start(dst.rearrange("(p t) d -> p (t d)", p=NP_), src[:, :]).then_inc(n_store.sem, 16)
                        sp.wait_ge(n_store.sem, n_store.at(16))

                    @block.vector
                    def _(eng):
                        run("dve", eng)

                    @block.scalar
                    def _(eng):
                        run("act", eng)

                    @block.tensor
                    def _(eng):
                        run("pe", eng)
                for k_, c_ in counters.items():
                    c_.base = number[k_]
                if n:
                    for c_ in n_part:
                        c_.base += 16 * (NT // NCH)
                n_store.base += 16

        srcT, dstT = a["srcT"], a["dstT"]
        node_stage(0)
        edge_pass(0, srcT, dstT, ew_d=a["ewT"])
        node_stage(1)
        edge_pass(1, dstT, srcT, ea_d=a["eaT"])
        node_stage(2)
        edge_pass(2, srcT, dstT)
        node_stage(3)
        edge_pass(3, dstT, srcT)
        node_stage(4, last=True)


def kernel(**inputs):
    import numpy as _np
    import concourse.bacc as _bacc
    from concourse import mybir as _mybir
    from concourse.bass_utils import run_bass_kernel_spmd as _run

    nc = _bacc.Bacc("TRN2", target_bir_lowering=False, num_devices=1)
    i = {k: _np.asarray(v) for k, v in inputs.items()}
    laid = {
        "x": i["x"],
        "srcT": i["src"].reshape(TILES, P).T,
        "dstT": i["dst"].reshape(TILES, P).T,
        "ewT": i["edge_weight"].reshape(TILES, P).T,
        "eaT": i["edge_attr_64"].T,
        "L0_gnn_W": i["L0_gnn_W"],
        "WlT": i["L1_gnn_Wl"].T, "bl": i["L1_gnn_bl"].reshape(1, D),
        "Wf1T": i["L1_gnn_Wf1"].T, "bf1": i["L1_gnn_bf1"].reshape(D, 1),
        "Wf2T": i["L1_gnn_Wf2"].T, "bf2": i["L1_gnn_bf2"].reshape(1, D),
        "L2_gnn_W1": i["L2_gnn_W1"], "b1": i["L2_gnn_b1"].reshape(D, 1),
        "L2_gnn_W2": i["L2_gnn_W2"], "b2": i["L2_gnn_b2"].reshape(1, D),
        "L3_gnn_weight": i["L3_gnn_weight"],
        "gamma": i["L1_gnn_gamma"].reshape(1, D), "beta": i["L1_gnn_beta"].reshape(1, D),
        "bias3": i["L3_gnn_bias"].reshape(1, D),
    }
    arrays, args = {}, {}
    for name, v in laid.items():
        v = _np.ascontiguousarray(v)
        arrays[f"in_{name}"] = v
        args[name] = nc.dram_tensor(f"in_{name}", v.shape, _mybir.dt.from_np(v.dtype), kind="ExternalInput").ap()
    out = nc.dram_tensor("out_rows", (NODES, D), _mybir.dt.float32, kind="ExternalOutput").ap()
    build(nc, args, out)
    r = _run(nc, [arrays], core_ids=[0])
    return r.results[0]["out_rows"]
```

```python
import numpy as np
import concourse.bass as bass
from concourse import mybir
from contextlib import ExitStack

F32 = mybir.dt.float32
I32 = mybir.dt.int32
ALU = mybir.AluOpType
ACT = mybir.ActivationFunctionType
AX = mybir.AxisListType

NODES, EDGES, D = 12500, 400000, 64
P = 128
TILES = EDGES // P
GROUP = 25
TURNS = TILES // GROUP
CHUNK = 5
CHUNKS = GROUP // CHUNK
TABLES = CHUNK
AHEAD = 10
HALVES = ((0, 10), (10, 25))
NT = 100
ROWS = P * NT
PROWS = ROWS + P
ZR = -(-(PROWS // P) // CHUNK)
SHIFT = 7
BF16 = mybir.dt.bfloat16
CREDIT = 5
NCH = 20
QUAD = 4
EPS = 1e-5


class Counter:

    def __init__(self, sem):
        self.sem, self.base = sem, 0

    def at(self, n):
        return n + self.base


def build(nc, a, out):
    ctx = ExitStack()
    with ctx:
        def sb(name, shape, dt=F32):
            return ctx.enter_context(nc.sbuf_tensor(name, shape, dt))

        def ps(name):
            return ctx.enter_context(nc.psum_tensor(name, [P, 512], F32))

        def counter(name):
            return Counter(ctx.enter_context(nc.semaphore(name)))

        table = [nc.dram_tensor(f"node_table_{n}", (ROWS, D), F32, kind="Internal").ap() for n in range(4)]
        width = [D, D + 1, D, D]
        part = [[nc.dram_tensor(f"partial_{n}_{k}", (PROWS, width[n]), F32, kind="Internal").ap()
                 for k in range(TABLES)] for n in range(4)]
        row_d, rowf_d, rowhl_d = ([nc.dram_tensor(f"{what}_{x}", (P, TILES * m), dt, kind="Internal").ap()
                                   for x in ("src", "dst")]
                                  for what, dt, m in (("row", I32, 1),
                                                      ("rowf", F32, 1),
                                                      ("rowhl", BF16, 2)))
        nearf_d = nc.dram_tensor("near", (P, TILES), F32, kind="Internal").ap()
        nearb_d = nc.dram_tensor("near_b", (P, TILES), BF16, kind="Internal").ap()

        ident = sb("ident", [P, P])
        upper = sb("upper", [P, P])
        identb = sb("identb", [P, P], BF16)
        iota2 = sb("iota2", [P, 2])
        iotaw = sb("iotaw", [P, 2 * P])
        ones = sb("ones", [P, P])
        flag = sb("flag", [1, 2], I32)
        base = sb("base", [1, TURNS], I32)
        trash = sb("trash", [P, 1])
        zeros = sb("zeros", [P, ZR * (D + 1)])
        w0 = sb("w0", [D, D])
        wl = sb("wl", [D + 1, D])
        wf1 = sb("wf1", [D, D])
        bf1 = sb("bf1", [D, 1])
        wf2 = sb("wf2", [D + 1, D])
        w1 = sb("w1", [D, D])
        b1 = sb("b1", [D, 1])
        w2 = sb("w2", [D + 1, D])
        w3 = sb("w3", [D, D])
        gamma = sb("gamma", [P, D])
        beta = sb("beta", [P, D])
        bias3 = sb("bias3", [P, D])

        xr = sb("x_rows", [P, NT * D])
        tab = sb("tab", [P, NT, D])
        acc = sb("acc", [P, NT, D])
        dinv = sb("dinv", [P, NT])

        psb = [ps(f"ps_{n}") for n in range(8)]

        settled = ctx.enter_context(nc.semaphore("settled"))
        s_const = counter("s_const")
        s_load = counter("s_load")

        def settle(eng):
            eng.sem_inc(settled, 1)

        loads = [(w0[:, :], a["L0_gnn_W"]), (wl[0:D, :], a["WlT"]), (wl[D:D + 1, :], a["bl"]),
                 (wf1[:, :], a["Wf1T"]), (bf1[:, :], a["bf1"]), (wf2[0:D, :], a["Wf2T"]), (wf2[D:D + 1, :], a["bf2"]),
                 (w1[:, :], a["L2_gnn_W1"]), (b1[:, :], a["b1"]), (w2[0:D, :], a["L2_gnn_W2"]), (w2[D:D + 1, :], a["b2"]),
                 (w3[:, :], a["L3_gnn_weight"]),
                 (gamma[:, :], a["gamma"].to_broadcast([P, D])), (beta[:, :], a["beta"].to_broadcast([P, D])),
                 (bias3[:, :], a["bias3"].to_broadcast([P, D])),
                 (xr[:, :], a["x"])]

        with nc.Block() as block:
            @block.sync
            def _(sp):
                for dst, src in loads:
                    sp.dma_start(dst, src).then_inc(s_load.sem, 16)
                sp.wait_ge(s_load.sem, 16 * len(loads))

            @block.gpsimd
            def _(pool):
                pool.memset(ident[:, :], 0.0).then_inc(s_const.sem, 1)
                pool.memset(upper[:, :], 1.0).then_inc(s_const.sem, 1)
                pool.memset(zeros[:, :], 0.0).then_inc(s_const.sem, 1)
                pool.memset(ones[:, :], 1.0).then_inc(s_const.sem, 1)
                pool.iota(iota2[:, :], pattern=[[P, 2]], base=0, channel_multiplier=1,
                          allow_small_or_imprecise_dtypes=True).then_inc(s_const.sem, 1)
                pool.iota(iotaw[:, :], pattern=[[1, 2 * P]], base=0, channel_multiplier=0,
                          allow_small_or_imprecise_dtypes=True).then_inc(s_const.sem, 1)
                pool.iota(trash[:, :], pattern=[[0, 1]], base=ROWS, channel_multiplier=1,
                          allow_small_or_imprecise_dtypes=True).then_inc(s_const.sem, 1)
                pool.wait_ge(s_const.sem, 7)
                pool.affine_select(out=ident[:, :], in_=ident[:, :], compare_op=ALU.not_equal, fill=1.0,
                                   base=0, pattern=[[-1, P]], channel_multiplier=1).then_inc(s_const.sem, 1)
                pool.affine_select(out=upper[:, :], in_=upper[:, :], compare_op=ALU.is_ge, fill=0.0,
                                   base=0, pattern=[[1, P]], channel_multiplier=-1).then_inc(s_const.sem, 1)
                pool.wait_ge(s_const.sem, 9)
                pool.tensor_copy(identb[:, :], ident[:, :]).then_inc(s_const.sem, 1)
                pool.wait_ge(s_const.sem, 10)

        def index_stage():
            ictx = ExitStack()
            with ictx:
                def sbi(name, shape, dt=F32):
                    return ictx.enter_context(nc.sbuf_tensor(name, shape, dt))
                raw = [sbi(f"raw_{x}", [P, TILES], I32)[:, :] for x in range(2)]
                hi, lo = sbi("hi", [P, TILES], I32), sbi("lo", [P, TILES], I32)
                row = [sbi(f"row_{x}", [P, TILES], I32) for x in range(2)]
                rowf = [raw[0].bitcast(F32) if x == 0 else sbi("rowf_1", [P, TILES]) for x in range(2)]
                rowhl = [sbi(f"rowhl_{x}", [P, TILES, 2], BF16) for x in range(2)]
                basef = sbi("basef", [1, TURNS])
                nearf = hi[:, :].bitcast(F32)
                nearb = sbi("nearb", [P, TILES], BF16)
                lim = sbi("lim", [P, 4])
                i_in, i_out, i_dve, i_pe = (ictx.enter_context(nc.semaphore(x)) for x in ("i_in", "i_out", "i_dve", "i_pe"))
                marks = {}
                with nc.Block() as block:
                    @block.vector
                    def _(dve):
                        n = [0]

                        def step(i, name=None):
                            i.then_inc(i_dve, 1)
                            n[0] += 1
                            dve.wait_ge(i_dve, n[0])
                            if name:
                                marks[name] = n[0]
                        dve.wait_ge(i_in, 32)
                        for x in (1, 0):
                            step(dve.tensor_scalar(hi[:, :], raw[x][:, :], SHIFT, None, ALU.logical_shift_right))
                            step(dve.tensor_scalar(lo[:, :], raw[x][:, :], P - 1, None, ALU.bitwise_and))
                            if x == 1:
                                first = hi[0:1, :].rearrange("p (r j) -> p r j", j=GROUP)[:, :, 0]
                                step(dve.tensor_copy(base[:, :], first))
                                step(dve.tensor_copy(basef[:, :], first), "basef")
                            step(dve.scalar_tensor_tensor(out=row[x][:, :], in0=lo[:, :], scalar=float(NT), in1=hi[:, :],
                                                          op0=ALU.mult, op1=ALU.add))
                            step(dve.tensor_copy(rowf[x][:, :], row[x][:, :]))
                            step(dve.tensor_scalar(hi[:, :], row[x][:, :], SHIFT, SHIFT,
                                                   ALU.logical_shift_right, ALU.logical_shift_left))
                            step(dve.tensor_copy(rowhl[x][:, :, 0], hi[:, :]))
                            step(dve.tensor_scalar(lo[:, :], row[x][:, :], P - 1, None, ALU.bitwise_and))
                            step(dve.tensor_copy(rowhl[x][:, :, 1], lo[:, :]), f"rows{x}")
                        dve.wait_ge(i_pe, 1)
                        bb = psb[0][:, 0:TURNS].unsqueeze(2).to_broadcast([P, TURNS, GROUP])
                        view = [v.rearrange("p (r j) -> p r j", j=GROUP) for v in (nearf[:, :], raw[1][:, :])]
                        step(dve.scalar_tensor_tensor(out=view[0], in0=bb, scalar=-float(P), in1=view[1],
                                                      op0=ALU.mult, op1=ALU.add))
                        step(dve.tensor_copy(nearb[:, :], nearf[:, :]), "near")
                        step(dve.tensor_reduce(lim[:, 0:1], nearf[:, :], AX.X, ALU.min))
                        step(dve.tensor_reduce(lim[:, 1:2], nearf[:, :], AX.X, ALU.max))
                        step(dve.tensor_scalar(lim[:, 2:3], lim[:, 0:1], -0.5, None, ALU.is_lt))
                        step(dve.scalar_tensor_tensor(out=lim[:, 3:4], in0=lim[:, 1:2], scalar=2 * P - 0.5, in1=lim[:, 2:3],
                                                      op0=ALU.is_gt, op1=ALU.add), "outside")
                        dve.wait_ge(i_pe, 2)
                        step(dve.tensor_scalar(flag[:, 0:1], psb[1][0:1, 0:1], 0.5, None, ALU.is_lt))
                        step(dve.tensor_scalar(flag[:, 1:2], psb[1][0:1, 0:1], 0.5, None, ALU.is_gt))

                    @block.tensor
                    def _(pe):
                        pe.wait_ge(i_dve, marks["basef"])
                        pe.matmul(psb[0][:, 0:TURNS], ones[0:1, :], basef[:, :], start=True, stop=True).then_inc(i_pe, 1)
                        pe.wait_ge(i_dve, marks["outside"])
                        pe.matmul(psb[1][0:1, 0:1], lim[:, 3:4], ones[:, 0:1], start=True, stop=True).then_inc(i_pe, 1)

                    @block.sync
                    def _(sp):
                        sp.dma_start(raw[1][:, :], a["dstT"]).then_inc(i_in, 16)
                        sp.dma_start(raw[0][:, :], a["srcT"]).then_inc(i_in, 16)
                        stores = 0
                        for x in (1, 0):
                            sp.wait_ge(i_dve, marks[f"rows{x}"])
                            for dst, src in ((row_d[x], row[x][:, :]), (rowf_d[x], rowf[x][:, :]),
                                             (rowhl_d[x], rowhl[x][:, :, :].rearrange("p t m -> p (t m)"))):
                                sp.dma_start(dst, src).then_inc(i_out, 16)
                                stores += 1
                        sp.wait_ge(i_dve, marks["near"])
                        for dst, src in ((nearf_d, nearf), (nearb_d, nearb)):
                            sp.dma_start(dst, src[:, :]).then_inc(i_out, 16)
                            stores += 1
                        sp.wait_ge(i_out, 16 * stores)

        def under(eng, which):
            return eng.If(eng.value_load(flag[0:1, which:which + 1], min_val=0, max_val=1))

        def fill_piece(n, k, q):
            W, rows = width[n], PROWS // P
            lo, hi = q * ZR, min((q + 1) * ZR, rows)
            return part[n][k].rearrange("(p a) w -> p (a w)", p=P)[:, lo * W:hi * W], (hi - lo) * W

        def half_of(c):
            return 0 if c * CHUNK < HALVES[0][1] else 1

        def wait(eng, cnt_, r, n_, per=CHUNKS, credit=CREDIT):
            eng.wait_ge(cnt_.sem, r * per + (cnt_.at(credit + n_)))

        def dma_wait(eng, cnt_, r):
            eng.wait_ge(cnt_.sem, r * 16 + cnt_.at(16))

        def cols(src, r, h, m=1):
            lo, hi = HALVES[h]
            return src[:, bass.ds(r * (GROUP * m) + lo * m, (hi - lo) * m)]

        s_tabd = counter("tab_in_dram")

        sem_gidx = [counter(f"gidx_in_{h}") for h in range(2)]
        sem_sidx = [counter(f"sidx_in_{h}") for h in range(2)]
        sem_ew = [counter(f"ew_in_{h}") for h in range(2)]
        sem_ea = [counter(f"ea_in_{h}") for h in range(2)]
        sem_gath = [counter(f"gathered_{j}") for j in range(GROUP)]
        sem_tab = [counter(f"added_{k}") for k in range(TABLES)]
        sem_hl = [counter(f"hl_in_{h}") for h in range(2)]
        s_bc = counter("bcast_done")
        s_sel = counter("sel_done")
        s_tr = counter("trash_done")
        s_fin = counter("fin_done")
        s_msg = counter("msg_done")
        s_f1 = counter("f1_done")
        s_h = counter("silu_done")
        s_f2 = counter("f2_done")
        s_mg = counter("merge_done")
        s_out = counter("out_done")

        def far_pass(n, gx, sx, ew_d=None, ea_d=None):
            W = width[n]
            made = ew_d is not None or ea_d is not None
            ectx = ExitStack()
            with ectx:
                def sbe(name, shape, dt=F32):
                    return ectx.enter_context(nc.sbuf_tensor(f"{name}_{n}", shape, dt))

                gidx = sbe("gidx", [P, GROUP], I32)
                idxf = sbe("idxf", [P, GROUP])
                hl = sbe("hl", [P, GROUP, 2], BF16)
                cnt = sbe("cnt", [P, GROUP])
                off = sbe("off", [P, GROUP])
                fin = sbe("fin", [P, GROUP], I32)
                ew = sbe("ew", [P, GROUP])
                g = sbe("g", [P, GROUP, D])
                msg = sbe("msg", [P, GROUP, W]) if made else g
                sel = sbe("sel", [P, GROUP, P])
                o = sbe("o", [P, GROUP, W])
                ea = sbe("ea", [D, GROUP * P]) if ea_d is not None else None
                hT = sbe("hT", [D + 1, CHUNK * P]) if ea_d is not None else None

                def bc(k):
                    return psb[k // 4][:, (k % 4) * P:(k % 4 + 1) * P]

                HC = CHUNK * P // 2
                merged = psb[2][:, 0:CHUNK * W]
                f2 = psb[3][:, 0:CHUNK * D]
                f1 = [psb[4][0:D, 0:HC], psb[5][0:D, 0:HC]]

                def load_half(sp, h, r):
                    lo, hi = HALVES[h]

                    def cols(src):
                        return src[:, bass.ds(r * GROUP + lo, hi - lo)]
                    sp.dma_start(gidx[:, lo:hi], cols(row_d[gx])).then_inc(sem_gidx[h].sem, 16)
                    sp.dma_start(idxf[:, lo:hi], cols(rowf_d[sx])).then_inc(sem_sidx[h].sem, 16)
                    sp.dma_start(hl[:, lo:hi, :].rearrange("p t m -> p (t m)"),
                                 rowhl_d[sx][:, bass.ds(r * (2 * GROUP) + 2 * lo, 2 * (hi - lo))]).then_inc(sem_hl[h].sem, 16)
                    if ew_d is not None:
                        sp.dma_start(ew[:, lo:hi], cols(ew_d)).then_inc(sem_ew[h].sem, 16)
                    if ea_d is not None:
                        sp.dma_start(ea[:, lo * P:hi * P], ea_d[:, bass.ds(r * (GROUP * P) + lo * P, (hi - lo) * P)])\
                            .then_inc(sem_ea[h].sem, 16)

                def half_of(c):
                    return 0 if c * CHUNK < HALVES[0][1] else 1

                def tables_free(eng, r, c):
                    for k in range(TABLES):
                        eng.wait_ge(sem_tab[k].sem, sem_tab[k].at(16 * (CREDIT * r + c + 1)) if isinstance(r, int)
                                    else r * (16 * CREDIT) + sem_tab[k].at(16 * (c + 1)))

                def wait(eng, cnt_, r, n_, per=CHUNKS, credit=CREDIT):
                    eng.wait_ge(cnt_.sem, r * per + (cnt_.at(credit + n_)))

                with nc.Block() as block:
                    @block.sync
                    def _(sp):
                        with under(sp, 1):
                          if n in (1, 3):
                              sp.dma_start(table[n].rearrange("(p t) d -> p (t d)", p=P), tab[:, :, :].rearrange("p t d -> p (t d)"))\
                                  .then_inc(s_tabd.sem, 16)
                          for h in range(2):
                              load_half(sp, h, 0)

                          def body(r):
                              for h in range(2):
                                  wait(sp, s_mg, r, HALVES[h][1] // CHUNK)
                                  settle(sp)
                                  wait(sp, s_fin, r, HALVES[h][1] // CHUNK)
                                  settle(sp)
                                  load_half(sp, h, r + 1)
                          with sp.Fori(0, TURNS - 1) as r:
                              body(r)

                    @block.gpsimd
                    def _(pool):
                        with under(pool, 1):
                          def gather(j, r):
                              c = j // CHUNK
                              h = half_of(c)
                              if j % CHUNK == 0:
                                  pool.wait_ge(sem_gidx[h].sem, r * 16 + sem_gidx[h].at(16))
                                  wait(pool, s_mg, r, c + 1 - CHUNKS)
                                  settle(pool)
                              pool.indirect_dma_start(
                                  out=g[:, j, :], out_offset=None, in_=table[n],
                                  in_offset=bass.IndirectOffsetOnAxis(ap=gidx[:, j:j + 1], axis=0))\
                                  .then_inc(sem_gath[j].sem, 16)

                          def scatter(j, r):
                              c, k = divmod(j, CHUNK)
                              if k == 0:
                                  wait(pool, s_out, r, c + 1)
                                  wait(pool, s_fin, r, c + 1)
                              pool.wait_ge(sem_tab[k].sem, r * (16 * CHUNKS) + sem_tab[k].at(16 * (CREDIT + c)))
                              settle(pool)
                              pool.indirect_dma_start(
                                  out=part[n][k], out_offset=bass.IndirectOffsetOnAxis(ap=fin[:, j:j + 1], axis=0),
                                  in_=o[:, j, :], in_offset=None, compute_op=ALU.add)\
                                  .then_inc(sem_tab[k].sem, 16)

                          for q in range(CREDIT):
                              for k in range(TABLES):
                                  if q:
                                      pool.wait_ge(sem_tab[k].sem, sem_tab[k].at(16 * q))
                                  dst, m = fill_piece(n, k, q)
                                  pool.dma_start(dst, zeros[:, 0:m]).then_inc(sem_tab[k].sem, 16)
                          if n in (1, 3):
                              pool.wait_ge(s_tabd.sem, s_tabd.at(16))
                          for h in range(2):
                              pool.wait_ge(sem_gidx[h].sem, sem_gidx[h].at(16))
                          for j in range(AHEAD):
                              pool.indirect_dma_start(
                                  out=g[:, j, :], out_offset=None, in_=table[n],
                                  in_offset=bass.IndirectOffsetOnAxis(ap=gidx[:, j:j + 1], axis=0))\
                                  .then_inc(sem_gath[j].sem, 16)

                          def body(r, last):
                              for j in range(GROUP):
                                  ahead = j + AHEAD
                                  if ahead < GROUP:
                                      gather(ahead, r)
                                  elif not last:
                                      gather(ahead - GROUP, r + 1)
                                  scatter(j, r)
                          with pool.Fori(0, TURNS - 1) as r:
                              body(r, False)
                          body(TURNS - 1, True)
                          settle(pool)
                          for k in range(TABLES):
                              pool.wait_ge(sem_tab[k].sem, sem_tab[k].at(16 * CHUNKS * (TURNS + 1)))

                    @block.vector
                    def _(dve):
                        with under(dve, 1):
                          for s in (s_sel, s_tr, s_fin, s_msg):
                              dve.sem_inc(s.sem, CREDIT)
                          if ea_d is not None:
                              dve.memset(msg[:, :, D:D + 1], 1.0).then_inc(s_h.sem, 1)

                          def body(r):
                              for c in range(CHUNKS):
                                  lo, hi = c * CHUNK, (c + 1) * CHUNK
                                  h = half_of(c)
                                  if lo == HALVES[h][0]:
                                      dve.wait_ge(sem_sidx[h].sem, r * 16 + sem_sidx[h].at(16))
                                  wait(dve, s_bc, r, c + 1)
                                  wait(dve, s_mg, r, c + 1 - CHUNKS)
                                  wait(dve, s_tr, r, c + 1 - CHUNKS)
                                  settle(dve)
                                  for j in range(lo, hi):
                                      i = dve.scalar_tensor_tensor(
                                          out=sel[:, j, :], in0=bc(j - lo), scalar=idxf[:, j:j + 1], in1=upper[:, :],
                                          op0=ALU.is_equal, op1=ALU.mult, accum_out=cnt[:, j:j + 1])
                                  i.then_inc(s_sel.sem, 1)
                                  wait(dve, s_sel, r, c + 1)
                                  wait(dve, s_fin, r, c + 1 - CHUNKS)
                                  settle(dve)
                                  dve.tensor_scalar(off[:, lo:hi], cnt[:, lo:hi], 1.5, trash[:, 0:1], ALU.is_gt, ALU.mult)\
                                      .then_inc(s_tr.sem, 1)
                                  wait(dve, s_tr, r, c + 1)
                                  tables_free(dve, r, c)
                                  settle(dve)
                                  dve.tensor_tensor(fin[:, lo:hi], off[:, lo:hi], idxf[:, lo:hi], ALU.max)\
                                      .then_inc(s_fin.sem, 1)
                                  if not made:
                                      continue
                                  for j in range(lo, hi):
                                      dve.wait_ge(sem_gath[j].sem, r * 16 + sem_gath[j].at(16))
                                  if ew_d is not None:
                                      dve.wait_ge(sem_ew[h].sem, r * 16 + sem_ew[h].at(16))
                                      wait(dve, s_mg, r, c + 1 - CHUNKS)
                                      settle(dve)
                                      dve.tensor_tensor(msg[:, lo:hi, :], g[:, lo:hi, :],
                                                        ew[:, lo:hi].unsqueeze(2).to_broadcast([P, CHUNK, D]), ALU.mult)\
                                          .then_inc(s_msg.sem, 1)
                                  else:
                                      wait(dve, s_f2, r, c + 1)
                                      settle(dve)
                                      dve.tensor_tensor(msg[:, lo:hi, 0:D], g[:, lo:hi, :],
                                                        f2.rearrange("p (k d) -> p k d", d=D), ALU.mult)\
                                          .then_inc(s_msg.sem, 1)
                          with dve.Fori(0, TURNS) as r:
                              body(r)

                    @block.tensor
                    def _(pe):
                        with under(pe, 1):
                          for s in (s_bc, s_f1, s_f2, s_mg):
                              pe.sem_inc(s.sem, CREDIT)

                          def body(r):
                              for c in range(CHUNKS):
                                  lo, hi = c * CHUNK, (c + 1) * CHUNK
                                  h = half_of(c)
                                  if lo == HALVES[h][0]:
                                      pe.wait_ge(sem_hl[h].sem, r * 16 + sem_hl[h].at(16))
                                  wait(pe, s_sel, r, c)
                                  settle(pe)
                                  for j in range(lo, hi):
                                      for m in range(2):
                                          i = pe.matmul(bc(j - lo), hl[:, j, m:m + 1].to_broadcast([P, P]), identb[:, :],
                                                        start=(m == 0), stop=(m == 1))
                                  i.then_inc(s_bc.sem, 1)
                                  if ea_d is not None:
                                      pe.wait_ge(sem_ea[h].sem, r * 16 + sem_ea[h].at(16))
                                      wait(pe, s_h, r, c)
                                      settle(pe)
                                      for b in range(2):
                                          i = pe.matmul(f1[b], wf1[:, :], ea[:, lo * P + b * HC:lo * P + (b + 1) * HC],
                                                        start=True, stop=True)
                                      i.then_inc(s_f1.sem, 1)
                                      wait(pe, s_h, r, c + 1)
                                      wait(pe, s_msg, r, c)
                                      settle(pe)
                                      for k in range(CHUNK):
                                          i = pe.matmul(f2[:, k * D:(k + 1) * D], hT[:, k * P:(k + 1) * P], wf2[:, :],
                                                        start=True, stop=True)
                                      i.then_inc(s_f2.sem, 1)
                                  wait(pe, s_sel, r, c + 1)
                                  wait(pe, s_out, r, c)
                                  if made:
                                      wait(pe, s_msg, r, c + 1)
                                  else:
                                      for j in range(lo, hi):
                                          pe.wait_ge(sem_gath[j].sem, r * 16 + sem_gath[j].at(16))
                                  settle(pe)
                                  for j in range(lo, hi):
                                      k = j - lo
                                      i = pe.matmul(merged[:, k * W:(k + 1) * W], sel[:, j, :], msg[:, j, :],
                                                    start=True, stop=True)
                                  i.then_inc(s_mg.sem, 1)
                          with pe.Fori(0, TURNS) as r:
                              body(r)

                    @block.scalar
                    def _(act):
                        with under(act, 1):
                          act.sem_inc(s_out.sem, CREDIT)
                          if ea_d is not None:
                              act.activation(hT[D:D + 1, :], zeros[0:1, 0:CHUNK * P], ACT.Copy, bias=1.0).then_inc(s_h.sem, CREDIT - 1)

                          def body(r):
                              for c in range(CHUNKS):
                                  lo, hi = c * CHUNK, (c + 1) * CHUNK
                                  if ea_d is not None:
                                      wait(act, s_f1, r, c + 1)
                                      wait(act, s_f2, r, c)
                                      settle(act)
                                      for b in range(2):
                                          i = act.activation(hT[0:D, b * HC:(b + 1) * HC], f1[b], ACT.Silu, bias=bf1[:, 0:1])
                                      i.then_inc(s_h.sem, 1)
                                  wait(act, s_mg, r, c + 1)
                                  tables_free(act, r, c)
                                  settle(act)
                                  act.activation(o[:, lo:hi, :], merged.rearrange("p (k w) -> p k w", w=W), ACT.Copy)\
                                      .then_inc(s_out.sem, 1)
                          with act.Fori(0, TURNS) as r:
                              body(r)

            for c_ in sem_gidx + sem_sidx + sem_hl + sem_gath:
                c_.base += 16 * TURNS
            if ew_d is not None:
                for c_ in sem_ew:
                    c_.base += 16 * TURNS
            if ea_d is not None:
                for c_ in sem_ea:
                    c_.base += 16 * TURNS
                for c_ in (s_f1, s_h, s_f2):
                    c_.base += CHUNKS * TURNS + CREDIT
            else:
                for c_ in (s_f1, s_f2):
                    c_.base += CREDIT
            for c_ in sem_tab:
                c_.base += 16 * CHUNKS * (TURNS + 1)
            if n in (1, 3):
                s_tabd.base += 16
            for c_ in (s_sel, s_tr, s_fin, s_bc, s_mg, s_out):
                c_.base += CHUNKS * TURNS + CREDIT
            s_msg.base += (CHUNKS * TURNS if made else 0) + CREDIT

        def far_collect(n):
            cctx = ExitStack()
            with cctx:
                pin = [cctx.enter_context(nc.sbuf_tensor(f"fpin{k}_{n}", [P, NCH, D], F32)) for k in range(TABLES)]
                with nc.Block() as block:
                    @block.sync
                    def _(sp):
                        with under(sp, 1):
                            for q in range(NT // NCH):
                                if q:
                                    sp.wait_ge(f_sum.sem, f_sum.at(4 * q))
                                for k in range(TABLES):
                                    sp.dma_start(pin[k][:, :, :].rearrange("p a w -> p (a w)"),
                                                 part[n][k][0:ROWS, :].rearrange("(p a) w -> p (a w)", p=P)
                                                 [:, q * NCH * D:(q + 1) * NCH * D]).then_inc(f_part[k].sem, 16)

                    @block.vector
                    def _(dve):
                        with under(dve, 1):
                            for q in range(NT // NCH):
                                dst = acc[:, q * NCH:(q + 1) * NCH, :]
                                for k in range(TABLES):
                                    dve.wait_ge(f_part[k].sem, f_part[k].at(16 * (q + 1)))
                                for k in range(1, TABLES):
                                    dve.tensor_tensor(dst, pin[0][:, :, :] if k == 1 else dst, pin[k][:, :, :], ALU.add)\
                                        .then_inc(f_sum.sem, 1)
                                    dve.wait_ge(f_sum.sem, f_sum.at(4 * q + k))
            for c_ in f_part:
                c_.base += 16 * (NT // NCH)
            f_sum.base += 4 * (NT // NCH)

        f_part = [counter(f"far_part_{k}") for k in range(TABLES)]
        f_sum = counter("far_sum")

        m_gidx = [counter(f"m_gidx_in_{h}") for h in range(2)]
        m_near = [counter(f"m_near_in_{h}") for h in range(2)]
        m_ew = [counter(f"m_ew_in_{h}") for h in range(2)]
        m_ea = [counter(f"m_ea_in_{h}") for h in range(2)]
        m_rowf = [counter(f"m_rowf_in_{h}") for h in range(2)]
        m_hl = [counter(f"m_hl_in_{h}") for h in range(2)]
        m_gath = [counter(f"m_gathered_{j}") for j in range(GROUP)]
        m_tab = [counter(f"m_added_{k}") for k in range(TABLES)]
        m_fill = counter("m_filled")
        m_land = counter("m_landed")
        m_bc = counter("m_bcast_done")
        m_sel = counter("m_sel_done")
        m_tr = counter("m_trash_done")
        m_fin = counter("m_fin_done")
        m_msg = counter("m_msg_done")
        m_f1 = counter("m_f1_done")
        m_h = counter("m_silu_done")
        m_f2 = counter("m_f2_done")
        m_ex = counter("m_read_done")
        m_g = counter("m_copy_done")
        m_mg = counter("m_merge_done")
        m_out = counter("m_out_done")
        m_acc = counter("m_acc_done")

        def near_sum_pass(n, ew_d=None):
            ectx = ExitStack()
            with ectx:
                def sbe(name, shape, dt=F32):
                    return ectx.enter_context(nc.sbuf_tensor(f"m_{name}_{n}", shape, dt))
                gidx = sbe("gidx", [P, GROUP], I32)
                near = sbe("near", [P, GROUP])
                ew = sbe("ew", [P, GROUP])
                g = sbe("g", [P, GROUP, D])
                msg = sbe("msg", [P, GROUP, D]) if ew_d is not None else g
                hot = sbe("hot", [P, GROUP, 2 * P])
                psS = [psb[0][:, 0:D], psb[1][:, 0:D]]

                with nc.Block() as block:
                    @block.sync
                    def _(sp):
                        def load(r, h):
                            lo, hi = HALVES[h]
                            sp.dma_start(gidx[:, lo:hi], cols(row_d[0], r, h)).then_inc(m_gidx[h].sem, 16)
                            sp.dma_start(near[:, lo:hi], cols(nearf_d, r, h)).then_inc(m_near[h].sem, 16)
                            if ew_d is not None:
                                sp.dma_start(ew[:, lo:hi], cols(ew_d, r, h)).then_inc(m_ew[h].sem, 16)
                        with under(sp, 0):
                            for h in range(2):
                                load(0, h)
                            for q in range(CREDIT):
                                for k in range(TABLES):
                                    dst, m = fill_piece(n + 1, k, q)
                                    sp.dma_start(dst, zeros[:, 0:m]).then_inc(m_fill.sem, 16)
                            with sp.Fori(0, TURNS - 1) as r:
                                for h in range(2):
                                    wait(sp, m_mg, r, HALVES[h][1] // CHUNK)
                                    settle(sp)
                                    load(r + 1, h)
                            sp.wait_ge(m_fill.sem, m_fill.at(16 * CREDIT * TABLES))

                    @block.gpsimd
                    def _(pool):
                        with under(pool, 0):
                            with pool.Fori(0, TURNS) as r:
                                for j in range(GROUP):
                                    c = j // CHUNK
                                    if j % CHUNK == 0:
                                        dma_wait(pool, m_gidx[half_of(c)], r)
                                        wait(pool, m_mg, r, c + 1 - CHUNKS)
                                        settle(pool)
                                    pool.indirect_dma_start(
                                        out=g[:, j, :], out_offset=None, in_=table[n],
                                        in_offset=bass.IndirectOffsetOnAxis(ap=gidx[:, j:j + 1], axis=0))\
                                        .then_inc(m_gath[j].sem, 16)

                    @block.vector
                    def _(dve):
                        with under(dve, 0):
                            for s in (m_sel, m_acc) + ((m_msg,) if ew_d is not None else ()):
                                dve.sem_inc(s.sem, CREDIT)
                            dve.memset(acc[:, :, :], 0.0).then_inc(m_acc.sem, 1)
                            with dve.Fori(0, TURNS) as r:
                                b = dve.value_load(base[0:1, bass.ds(r, 1)], min_val=0, max_val=NT - 2)
                                for c in range(CHUNKS):
                                    lo, hi = c * CHUNK, (c + 1) * CHUNK
                                    h = half_of(c)
                                    dma_wait(dve, m_near[h], r)
                                    wait(dve, m_mg, r, c + 1 - CHUNKS)
                                    settle(dve)
                                    for j in range(lo, hi):
                                        i = dve.tensor_scalar(hot[:, j, :], iotaw[:, :], near[:, j:j + 1], None, ALU.is_equal)
                                    i.then_inc(m_sel.sem, 1)
                                    if ew_d is not None:
                                        for j in range(lo, hi):
                                            dma_wait(dve, m_gath[j], r)
                                        dma_wait(dve, m_ew[h], r)
                                        settle(dve)
                                        dve.tensor_tensor(msg[:, lo:hi, :], g[:, lo:hi, :],
                                                          ew[:, lo:hi].unsqueeze(2).to_broadcast([P, CHUNK, D]), ALU.mult)\
                                            .then_inc(m_msg.sem, 1)
                                wait(dve, m_mg, r, CHUNKS)
                                dve.wait_ge(m_acc.sem, r + m_acc.at(CREDIT + 1))
                                settle(dve)
                                for m in range(2):
                                    dst = acc[:, bass.ds(b + m, 1), :].rearrange("p o d -> p (o d)")
                                    i = dve.tensor_tensor(dst, dst, psS[m], ALU.add)
                                i.then_inc(m_acc.sem, 1)
                            dve.wait_ge(m_acc.sem, m_acc.at(CREDIT + 1 + TURNS))

                    @block.tensor
                    def _(pe):
                        with under(pe, 0):
                            pe.sem_inc(m_mg.sem, CREDIT)
                            with pe.Fori(0, TURNS) as r:
                                for c in range(CHUNKS):
                                    lo, hi = c * CHUNK, (c + 1) * CHUNK
                                    if c == 0:
                                        pe.wait_ge(m_acc.sem, r + m_acc.at(CREDIT + 1))
                                    wait(pe, m_sel, r, c + 1)
                                    if ew_d is not None:
                                        wait(pe, m_msg, r, c + 1)
                                    else:
                                        for j in range(lo, hi):
                                            dma_wait(pe, m_gath[j], r)
                                    settle(pe)
                                    for j in range(lo, hi):
                                        for m in range(2):
                                            i = pe.matmul(psS[m], hot[:, j, m * P:(m + 1) * P], msg[:, j, :],
                                                          start=(j == 0), stop=(j == GROUP - 1))
                                    i.then_inc(m_mg.sem, 1)
            for c_ in m_gidx + m_near + m_gath + (m_ew if ew_d is not None else []):
                c_.base += 16 * TURNS
            m_fill.base += 16 * CREDIT * TABLES
            for c_ in [m_sel, m_mg] + ([m_msg] if ew_d is not None else []):
                c_.base += CREDIT + CHUNKS * TURNS
            m_acc.base += CREDIT + 1 + TURNS

        def near_read_pass(n, ea_d=None):
            W = width[n]
            ectx = ExitStack()
            with ectx:
                def sbe(name, shape, dt=F32):
                    return ectx.enter_context(nc.sbuf_tensor(f"m_{name}_{n}", shape, dt))
                rowf = sbe("rowf", [P, GROUP])
                hl = sbe("hl", [P, GROUP, 2], BF16)
                nearb = sbe("nearb", [P, GROUP], BF16)
                cnt = sbe("cnt", [P, GROUP])
                off = sbe("off", [P, GROUP])
                fin = sbe("fin", [P, GROUP], I32)
                g = sbe("g", [P, GROUP, D])
                msg = sbe("msg", [P, GROUP, W]) if ea_d is not None else g
                sel = sbe("sel", [P, GROUP, P])
                hot = sbe("hot", [P, GROUP, 2, P])
                o = sbe("o", [P, GROUP, W])
                ea = sbe("ea", [D, GROUP * P]) if ea_d is not None else None
                hT = sbe("hT", [D + 1, CHUNK * P]) if ea_d is not None else None

                def row_of(k):
                    return psb[k // 4][:, (k % 4) * P:(k % 4 + 1) * P]

                HC = CHUNK * P // 2
                f1 = [psb[3][0:D, 0:HC], psb[4][0:D, 0:HC]]
                f2 = psb[5][:, 0:CHUNK * D]
                ex = psb[6][:, 0:CHUNK * D]
                merged = psb[7][:, 0:CHUNK * W]

                with nc.Block() as block:
                    @block.sync
                    def _(sp):
                        def load(r, h):
                            lo, hi = HALVES[h]
                            sp.dma_start(hl[:, lo:hi, :].rearrange("p t m -> p (t m)"), cols(rowhl_d[0], r, h, 2))\
                                .then_inc(m_hl[h].sem, 16)
                            sp.dma_start(nearb[:, lo:hi], cols(nearb_d, r, h)).then_inc(m_near[h].sem, 16)
                            sp.dma_start(rowf[:, lo:hi], cols(rowf_d[0], r, h)).then_inc(m_rowf[h].sem, 16)
                            if ea_d is not None:
                                sp.dma_start(ea[:, lo * P:hi * P], cols(ea_d, r, h, P)).then_inc(m_ea[h].sem, 16)
                        with under(sp, 0):
                            for h in range(2):
                                load(0, h)
                            with sp.Fori(0, TURNS - 1) as r:
                                for h in range(2):
                                    wait(sp, m_mg, r, HALVES[h][1] // CHUNK)
                                    settle(sp)
                                    wait(sp, m_fin, r, HALVES[h][1] // CHUNK)
                                    settle(sp)
                                    load(r + 1, h)

                    @block.gpsimd
                    def _(pool):
                        with under(pool, 0):
                            pool.sem_inc(m_land.sem, CREDIT - 1)
                            for k in range(TABLES):
                                pool.dma_start(part[n][k][ROWS:PROWS, :], zeros[:, 0:W]).then_inc(m_tab[k].sem, 16)
                            with pool.Fori(0, TURNS) as r:
                                for j in range(GROUP):
                                    c, k = divmod(j, CHUNK)
                                    if k == 0:
                                        wait(pool, m_out, r, c + 1)
                                        wait(pool, m_fin, r, c + 1)
                                    pool.wait_ge(m_tab[k].sem, r * (16 * CHUNKS) + m_tab[k].at(16 * (c + 1)))
                                    if k == TABLES - 1:
                                        pool.sem_inc(m_land.sem, 1)
                                    else:
                                        settle(pool)
                                    pool.indirect_dma_start(
                                        out=part[n][k], out_offset=bass.IndirectOffsetOnAxis(ap=fin[:, j:j + 1], axis=0),
                                        in_=o[:, j, :], in_offset=None, compute_op=ALU.add)\
                                        .then_inc(m_tab[k].sem, 16)
                            for k in range(TABLES):
                                pool.wait_ge(m_tab[k].sem, m_tab[k].at(16 * (CHUNKS * TURNS + 1)))

                    @block.vector
                    def _(dve):
                        def select(r, c):
                            lo, hi = c * CHUNK, (c + 1) * CHUNK
                            dma_wait(dve, m_rowf[half_of(c)], r)
                            wait(dve, m_bc, r, c + 1)
                            wait(dve, m_mg, r, c + 1 - CHUNKS)
                            wait(dve, m_tr, r, c + 1 - CHUNKS)
                            settle(dve)
                            for j in range(lo, hi):
                                dve.scalar_tensor_tensor(out=sel[:, j, :], in0=row_of(j - lo), scalar=rowf[:, j:j + 1],
                                                         in1=upper[:, :], op0=ALU.is_equal, op1=ALU.mult,
                                                         accum_out=cnt[:, j:j + 1])
                                for m in range(2):
                                    i = dve.tensor_scalar(hot[:, j, m, :], row_of(CHUNK + j - lo), iota2[:, m:m + 1], None,
                                                          ALU.is_equal)
                            i.then_inc(m_sel.sem, 1)
                            wait(dve, m_sel, r, c + 1)
                            wait(dve, m_fin, r, c + 1 - CHUNKS)
                            settle(dve)
                            dve.tensor_scalar(off[:, lo:hi], cnt[:, lo:hi], 1.5, trash[:, 0:1], ALU.is_gt, ALU.mult)\
                                .then_inc(m_tr.sem, 1)
                            wait(dve, m_tr, r, c + 1)
                            wait(dve, m_land, r, c + 1 - CHUNKS)
                            settle(dve)
                            dve.tensor_tensor(fin[:, lo:hi], off[:, lo:hi], rowf[:, lo:hi], ALU.max).then_inc(m_fin.sem, 1)

                        def body(r, last):
                            for c in range(CHUNKS):
                                lo, hi = c * CHUNK, (c + 1) * CHUNK
                                if c + 1 < CHUNKS:
                                    select(r, c + 1)
                                elif not last:
                                    select(r + 1, 0)
                                if ea_d is not None:
                                    wait(dve, m_f2, r, c + 1)
                                    wait(dve, m_g, r, c + 1)
                                    wait(dve, m_mg, r, c + 1 - CHUNKS)
                                    settle(dve)
                                    dve.tensor_tensor(msg[:, lo:hi, 0:D], g[:, lo:hi, :],
                                                      f2.rearrange("p (k d) -> p k d", d=D), ALU.mult)\
                                        .then_inc(m_msg.sem, 1)
                        with under(dve, 0):
                            for s in (m_sel, m_tr, m_fin):
                                dve.sem_inc(s.sem, CREDIT)
                            if ea_d is not None:
                                dve.memset(msg[:, :, D:D + 1], 1.0).then_inc(m_msg.sem, CREDIT)
                            select(0, 0)
                            with dve.Fori(0, TURNS - 1) as r:
                                body(r, False)
                            body(TURNS - 1, True)

                    @block.tensor
                    def _(pe):
                        def spread(r, c):
                            h = half_of(c)
                            dma_wait(pe, m_hl[h], r)
                            dma_wait(pe, m_near[h], r)
                            wait(pe, m_sel, r, c)
                            settle(pe)
                            for k in range(CHUNK):
                                j = c * CHUNK + k
                                for m in range(2):
                                    pe.matmul(row_of(k), hl[:, j, m:m + 1].to_broadcast([P, P]), identb[:, :],
                                              start=(m == 0), stop=(m == 1))
                                i = pe.matmul(row_of(CHUNK + k), nearb[:, j:j + 1].to_broadcast([P, P]), identb[:, :],
                                              start=True, stop=True)
                            i.then_inc(m_bc.sem, 1)

                        def merge(r, c):
                            wait(pe, m_msg if ea_d is not None else m_g, r, c + 1)
                            wait(pe, m_out, r, c)
                            settle(pe)
                            for k in range(CHUNK):
                                j = c * CHUNK + k
                                i = pe.matmul(merged[:, k * W:(k + 1) * W], sel[:, j, :], msg[:, j, :], start=True, stop=True)
                            i.then_inc(m_mg.sem, 1)

                        def body(r, last):
                            b = pe.value_load(base[0:1, bass.ds(r, 1)], min_val=0, max_val=NT - 2)
                            for c in range(CHUNKS):
                                lo, hi = c * CHUNK, (c + 1) * CHUNK
                                if c + 1 < CHUNKS:
                                    spread(r, c + 1)
                                elif not last:
                                    spread(r + 1, 0)
                                if ea_d is not None:
                                    dma_wait(pe, m_ea[half_of(c)], r)
                                    wait(pe, m_h, r, c)
                                    settle(pe)
                                    for q in range(2):
                                        i = pe.matmul(f1[q], wf1[:, :], ea[:, lo * P + q * HC:lo * P + (q + 1) * HC],
                                                      start=True, stop=True)
                                    i.then_inc(m_f1.sem, 1)
                                wait(pe, m_sel, r, c + 1)
                                wait(pe, m_g, r, c)
                                settle(pe)
                                for k in range(CHUNK):
                                    for m in range(2):
                                        i = pe.matmul(ex[:, k * D:(k + 1) * D], hot[:, lo + k, m, :],
                                                      tab[:, bass.ds(b + m, 1), :].rearrange("p o d -> p (o d)"),
                                                      start=(m == 0), stop=(m == 1))
                                i.then_inc(m_ex.sem, 1)
                                if ea_d is not None:
                                    wait(pe, m_h, r, c + 1)
                                    wait(pe, m_msg, r, c)
                                    settle(pe)
                                    for k in range(CHUNK):
                                        i = pe.matmul(f2[:, k * D:(k + 1) * D], hT[:, k * P:(k + 1) * P], wf2[:, :],
                                                      start=True, stop=True)
                                    i.then_inc(m_f2.sem, 1)
                                if c:
                                    merge(r, c - 1)
                            merge(r, CHUNKS - 1)
                        with under(pe, 0):
                            for s in (m_bc, m_ex, m_mg) + ((m_f1, m_f2) if ea_d is not None else ()):
                                pe.sem_inc(s.sem, CREDIT)
                            spread(0, 0)
                            with pe.Fori(0, TURNS - 1) as r:
                                body(r, False)
                            body(TURNS - 1, True)

                    @block.scalar
                    def _(act):
                        def sums(r, c):
                            wait(act, m_mg, r, c + 1)
                            wait(act, m_land, r, c + 1 - CHUNKS)
                            settle(act)
                            act.activation(o[:, c * CHUNK:(c + 1) * CHUNK, :], merged.rearrange("p (k w) -> p k w", w=W),
                                           ACT.Copy).then_inc(m_out.sem, 1)

                        with under(act, 0):
                            for s in (m_g, m_out):
                                act.sem_inc(s.sem, CREDIT)
                            if ea_d is not None:
                                act.activation(hT[D:D + 1, :], zeros[0:1, 0:CHUNK * P], ACT.Copy, bias=1.0).then_inc(m_h.sem, CREDIT)
                            with act.Fori(0, TURNS) as r:
                                for c in range(CHUNKS):
                                    lo, hi = c * CHUNK, (c + 1) * CHUNK
                                    if ea_d is not None:
                                        wait(act, m_f1, r, c + 1)
                                        wait(act, m_f2, r, c)
                                        settle(act)
                                        for q in range(2):
                                            i = act.activation(hT[0:D, q * HC:(q + 1) * HC], f1[q], ACT.Silu, bias=bf1[:, 0:1])
                                        i.then_inc(m_h.sem, 1)
                                    wait(act, m_ex, r, c + 1)
                                    wait(act, m_mg, r, c + 1 - CHUNKS)
                                    settle(act)
                                    act.activation(g[:, lo:hi, :], ex.rearrange("p (k d) -> p k d", d=D), ACT.Copy)\
                                        .then_inc(m_g.sem, 1)
                                    if c:
                                        sums(r, c - 1)
                                sums(r, CHUNKS - 1)
            for c_ in m_rowf + m_hl + m_near + (m_ea if ea_d is not None else []):
                c_.base += 16 * TURNS
            for c_ in m_tab:
                c_.base += 16 * (CHUNKS * TURNS + 1)
            m_land.base += CREDIT - 1 + CHUNKS * TURNS
            for c_ in [m_bc, m_sel, m_tr, m_fin, m_ex, m_g, m_mg, m_out] + ([m_f1, m_h, m_f2, m_msg] if ea_d is not None else []):
                c_.base += CREDIT + CHUNKS * TURNS

        n_dve = counter("node_dve")
        n_act = counter("node_act")
        n_pe = counter("node_pe")
        n_part = [counter(f"node_part_{k}") for k in range(TABLES)]
        n_store = counter("node_store")

        class Queue:

            def __init__(self, eng, count, start):
                self.eng, self.c, self.n = eng, count, start

            def step(self, i):
                i.then_inc(self.c.sem, 1)
                self.n += 1
                return self.n

        def node_stage(n, last=False):
            ectx = ExitStack()
            with ectx:
                def sbn(name, shape, dt=F32):
                    return ectx.enter_context(nc.sbuf_tensor(f"{name}_n{n}", shape, dt))
                W = width[n - 1] if n else D
                parts = n in (2, 4)
                pin = [sbn(f"pin{k}", [P, NCH, W]) for k in range(TABLES)] if parts else []
                y = sbn("y", [P, NCH, D])
                t = sbn("t", [P, NCH, D])
                st = sbn("st", [P, 6, NCH])
                xT = sbn("xT", [D + 1, QUAD * P])
                hT = sbn("hT", [D + 1, QUAD * P])
                xv = xr[:, :].rearrange("p (t d) -> p t d", d=D)
                tabv = tab[:, :, :]
                psT, psH, psO = psb[0], psb[1], psb[2]

                steps = []
                number = {"dve": n_dve.base, "act": n_act.base, "pe": n_pe.base}

                def do(name, waits, make):
                    number[name] += 1
                    steps.append((name, list(waits), make))
                    return (name, number[name])

                def dve(waits, make):
                    return do("dve", waits, make)

                prev = [None]

                def chain(make, extra=()):
                    w = ([prev[0]] if prev[0] else []) + list(extra)
                    prev[0] = dve(w, make)
                    return prev[0]

                def bcast(s, m=NCH):
                    return s.unsqueeze(2).to_broadcast([P, m, D])

                def rows(v, m=NCH):
                    return v.unsqueeze(1).to_broadcast([P, m, D])

                def norm(src, dst):
                    s0, s1, s2, s3 = (st[:, i, :] for i in range(4))
                    chain(lambda e: e.tensor_reduce(s0, src, AX.X, ALU.add))
                    chain(lambda e: e.tensor_scalar(s1, s0, 1.0 / D, None, ALU.mult))
                    chain(lambda e: e.tensor_tensor(src, src, bcast(s1), ALU.subtract))
                    chain(lambda e: e.tensor_tensor(t[:, :, :], src, src, ALU.mult))
                    chain(lambda e: e.tensor_reduce(s0, t[:, :, :], AX.X, ALU.add))
                    v = chain(lambda e: e.tensor_scalar(s2, s0, 1.0 / D, EPS, ALU.mult, ALU.add))
                    sd = do("act", [v], lambda e: e.activation(s3, s2, ACT.Sqrt))
                    chain(lambda e: e.reciprocal(s1, s3), [sd])
                    chain(lambda e: e.tensor_tensor(dst, src, bcast(s1), ALU.mult))

                def transposed(src_rows, after):
                    for m in range(QUAD):
                        p = do("pe", after, lambda e, m=m: e.transpose(psT[0:D, m * P:(m + 1) * P], src_rows[:, m, :],
                                                                      ident[0:P, 0:P]))
                    return do("act", [p], lambda e: e.activation(xT[0:D, :], psT[0:D, 0:QUAD * P], ACT.Copy))

                def product(wT, w, after):
                    k = w.shape[0]
                    for m in range(QUAD):
                        p = do("pe", after, lambda e, m=m: e.matmul(psO[0:P, m * D:(m + 1) * D], wT[0:k, m * P:(m + 1) * P],
                                                                    w, start=True, stop=True))
                    return p
                psOv = psO[0:P, 0:QUAD * D].rearrange("p (m d) -> p m d", d=D)

                ones = do("act", [], lambda e: e.activation(xT[D:D + 1, :], zeros[0:1, 0:QUAD * P], ACT.Copy, bias=1.0))
                ones = do("act", [], lambda e: e.activation(hT[D:D + 1, :], zeros[0:1, 0:QUAD * P], ACT.Copy, bias=1.0))
                part_read = []
                for q in range(NT // NCH if n else 0):
                    xq = xv[:, q * NCH:(q + 1) * NCH, :]
                    if parts:
                        chain(lambda e: e.tensor_tensor(pin[0][:, :, :], pin[0][:, :, :], pin[1][:, :, :], ALU.add),
                              [("part", 0, q), ("part", 1, q)])
                        for k in range(2, TABLES):
                            chain(lambda e, k=k: e.tensor_tensor(pin[0][:, :, :], pin[0][:, :, :], pin[k][:, :, :], ALU.add),
                                  [("part", k, q)])
                    agg = pin[0][:, :, 0:D] if parts else acc[:, q * NCH:(q + 1) * NCH, :]
                    if n == 1:
                        part_read.append(chain(lambda e, xq=xq, agg=agg: e.scalar_tensor_tensor(
                            out=y[:, :, :], in0=agg, scalar=0.0, in1=xq, op0=ALU.max, op1=ALU.add)))
                    elif n == 2:
                        deg, dv = pin[0][:, :, D], dinv[:, q * NCH:(q + 1) * NCH]
                        s4, s5 = st[:, 4, :], st[:, 5, :]
                        c1 = chain(lambda e, deg=deg: e.tensor_scalar(s4, deg, 1.0, None, ALU.max))
                        sd = do("act", [c1], lambda e: e.activation(s5, s4, ACT.Sqrt))
                        chain(lambda e: e.reciprocal(s4, s5), [sd])
                        chain(lambda e, deg=deg: e.tensor_scalar(s5, deg, 0.5, None, ALU.is_gt))
                        chain(lambda e, dv=dv: e.tensor_tensor(dv, s4, s5, ALU.mult))
                        part_read.append(chain(lambda e, xq=xq, agg=agg: e.tensor_tensor(y[:, :, :], agg, xq, ALU.add)))
                        norm(y[:, :, :], y[:, :, :])
                        chain(lambda e: e.tensor_tensor(y[:, :, :], y[:, :, :], rows(gamma[:, :]), ALU.mult))
                        chain(lambda e: e.tensor_tensor(y[:, :, :], y[:, :, :], rows(beta[:, :]), ALU.add))
                        chain(lambda e, xq=xq: e.tensor_tensor(y[:, :, :], y[:, :, :], xq, ALU.add))
                    elif n == 3:
                        part_read.append(chain(lambda e, xq=xq, agg=agg: e.tensor_tensor(y[:, :, :], agg, xq, ALU.add)))
                        for m in range(0, NCH, QUAD):
                            ax = transposed(y[:, m:m + QUAD, :], [prev[0], ones])
                            p = do("pe", [ax], lambda e: e.matmul(psH[0:D, 0:QUAD * P], w1[:, :], xT[0:D, :],
                                                                  start=True, stop=True))
                            ah = do("act", [p], lambda e: e.activation(hT[0:D, :], psH[0:D, 0:QUAD * P], ACT.Relu,
                                                                       bias=b1[:, 0:1]))
                            p = product(hT, w2[:, :], [ah])
                            chain(lambda e, m=m, xq=xq: e.tensor_tensor(y[:, m:m + QUAD, :], psOv, xq[:, m:m + QUAD, :], ALU.add),
                                  [p])
                    else:
                        dv = dinv[:, q * NCH:(q + 1) * NCH]
                        part_read.append(chain(lambda e, dv=dv, agg=agg: e.tensor_tensor(y[:, :, :], agg, bcast(dv), ALU.mult)))
                        chain(lambda e: e.tensor_tensor(y[:, :, :], y[:, :, :], rows(bias3[:, :]), ALU.add))
                        chain(lambda e, xq=xq: e.tensor_tensor(y[:, :, :], y[:, :, :], xq, ALU.add))
                    norm(y[:, :, :], xq)
                if n in (0, 1, 3):
                    w = {0: w0[:, :], 1: wl[:, :], 3: w3[:, :]}[n]
                    for m in range(0, NT, QUAD):
                        ax = transposed(xv[:, m:m + QUAD, :], [prev[0], ones] if prev[0] else [ones])
                        p = product(xT, w, [ax])
                        dst = tabv[:, m:m + QUAD, :]
                        if n == 3:
                            chain(lambda e, m=m, dst=dst: e.tensor_tensor(dst, psOv, bcast(dinv[:, m:m + QUAD], QUAD), ALU.mult), [p])
                        else:
                            chain(lambda e, dst=dst: e.tensor_copy(dst, psOv), [p])
                final = prev[0]
                src = tab[:, :, :].rearrange("p t d -> p (t d)") if n == 0 else xr[:, :]

                counters = {"dve": n_dve, "act": n_act, "pe": n_pe}

                def run(name, eng):
                    for who, waits, make in steps:
                        if who != name:
                            continue
                        for w in waits:
                            if w[0] == "part":
                                eng.wait_ge(n_part[w[1]].sem, n_part[w[1]].at(16 * (w[2] + 1)))
                            else:
                                eng.wait_ge(counters[w[0]].sem, w[1])
                        make(eng).then_inc(counters[name].sem, 1)

                with nc.Block() as block:
                    @block.sync
                    def _(sp):
                        for q in range(NT // NCH if parts else 0):
                            if q:
                                sp.wait_ge(n_dve.sem, part_read[q - 1][1])
                            for k in range(TABLES):
                                sp.dma_start(pin[k][:, :, :].rearrange("p a w -> p (a w)"),
                                             part[n - 1][k][0:ROWS, :].rearrange("(p a) w -> p (a w)", p=P)
                                             [:, q * NCH * W:(q + 1) * NCH * W]).then_inc(n_part[k].sem, 16)
                        sp.wait_ge(n_dve.sem, final[1])
                        if n in (0, 2, 4):
                            dst = out if last else table[n].rearrange("(p t) d -> p (t d)", p=P)
                            sp.dma_start(dst, src).then_inc(n_store.sem, 16)
                            sp.wait_ge(n_store.sem, n_store.at(16))

                    @block.vector
                    def _(eng):
                        run("dve", eng)

                    @block.scalar
                    def _(eng):
                        run("act", eng)

                    @block.tensor
                    def _(eng):
                        run("pe", eng)
                for k_, c_ in counters.items():
                    c_.base = number[k_]
                if parts:
                    for c_ in n_part:
                        c_.base += 16 * (NT // NCH)
                if n in (0, 2, 4):
                    n_store.base += 16

        index_stage()
        node_stage(0)
        near_sum_pass(0, ew_d=a["ewT"])
        far_pass(0, 0, 1, ew_d=a["ewT"])
        far_collect(0)
        node_stage(1)
        near_read_pass(1, ea_d=a["eaT"])
        far_pass(1, 1, 0, ea_d=a["eaT"])
        node_stage(2)
        near_sum_pass(2)
        far_pass(2, 0, 1)
        far_collect(2)
        node_stage(3)
        near_read_pass(3)
        far_pass(3, 1, 0)
        node_stage(4, last=True)


def kernel(**inputs):
    import numpy as _np
    import concourse.bacc as _bacc
    from concourse import mybir as _mybir
    from concourse.bass_utils import run_bass_kernel_spmd as _run

    nc = _bacc.Bacc("TRN2", target_bir_lowering=False, num_devices=1)
    i = {k: _np.asarray(v) for k, v in inputs.items()}
    laid = {
        "x": _np.pad(i["x"], ((0, ROWS - NODES), (0, 0))).reshape(NT, P, D).transpose(1, 0, 2).reshape(P, NT * D),
        "srcT": i["src"].reshape(TILES, P).T,
        "dstT": i["dst"].reshape(TILES, P).T,
        "ewT": i["edge_weight"].reshape(TILES, P).T,
        "eaT": i["edge_attr_64"].T,
        "L0_gnn_W": i["L0_gnn_W"],
        "WlT": i["L1_gnn_Wl"].T, "bl": i["L1_gnn_bl"].reshape(1, D),
        "Wf1T": i["L1_gnn_Wf1"].T, "bf1": i["L1_gnn_bf1"].reshape(D, 1),
        "Wf2T": i["L1_gnn_Wf2"].T, "bf2": i["L1_gnn_bf2"].reshape(1, D),
        "L2_gnn_W1": i["L2_gnn_W1"], "b1": i["L2_gnn_b1"].reshape(D, 1),
        "L2_gnn_W2": i["L2_gnn_W2"], "b2": i["L2_gnn_b2"].reshape(1, D),
        "L3_gnn_weight": i["L3_gnn_weight"],
        "gamma": i["L1_gnn_gamma"].reshape(1, D), "beta": i["L1_gnn_beta"].reshape(1, D),
        "bias3": i["L3_gnn_bias"].reshape(1, D),
    }
    arrays, args = {}, {}
    for name, v in laid.items():
        v = _np.ascontiguousarray(v)
        arrays[f"in_{name}"] = v
        args[name] = nc.dram_tensor(f"in_{name}", v.shape, _mybir.dt.from_np(v.dtype), kind="ExternalInput").ap()
    out = nc.dram_tensor("out_rows", (P, NT * D), _mybir.dt.float32, kind="ExternalOutput").ap()
    build(nc, args, out)
    r = _run(nc, [arrays], core_ids=[0])
    return r.results[0]["out_rows"].reshape(P, NT, D).transpose(1, 0, 2).reshape(ROWS, D)[:NODES]
```

```python
import numpy as np
import concourse.bass as bass
from concourse import mybir
from contextlib import ExitStack

F32 = mybir.dt.float32
I32 = mybir.dt.int32
ALU = mybir.AluOpType
ACT = mybir.ActivationFunctionType
AX = mybir.AxisListType

NODES, EDGES, D = 12500, 400000, 64
P = 128
TILES = EDGES // P
GROUP = 25
TURNS = TILES // GROUP
CHUNK = 5
CHUNKS = GROUP // CHUNK
TABLES = CHUNK
AHEAD = 10
HALVES = ((0, 10), (10, 25))
NT = 100
ROWS = P * NT
PROWS = ROWS + P
ZR = -(-(PROWS // P) // CHUNK)
SHIFT = 7
BF16 = mybir.dt.bfloat16
PARTS = 3
CREDIT = 5
NCH = 20
EPS = 1e-5


class Counter:

    def __init__(self, sem):
        self.sem, self.base = sem, 0

    def at(self, n):
        return n + self.base


def build(nc, a, out):
    ctx = ExitStack()
    with ctx:
        def sb(name, shape, dt=F32):
            return ctx.enter_context(nc.sbuf_tensor(name, shape, dt))

        def ps(name):
            return ctx.enter_context(nc.psum_tensor(name, [P, 512], F32))

        def counter(name):
            return Counter(ctx.enter_context(nc.semaphore(name)))

        table = [nc.dram_tensor(f"node_table_{n}", (ROWS, D), F32, kind="Internal").ap() for n in range(4)]
        width = [D, D + 1, D, D]
        part = [[nc.dram_tensor(f"partial_{n}_{k}", (PROWS, width[n]), F32, kind="Internal").ap()
                 for k in range(TABLES)] for n in range(4)]
        row_d, rowf_d = ([nc.dram_tensor(f"{what}_{x}", (P, TILES), dt, kind="Internal").ap() for x in ("src", "dst")]
                         for what, dt in (("row", I32), ("rowf", F32)))
        nearf_d = nc.dram_tensor("nearf", (P, TILES), F32, kind="Internal").ap()
        hl_d = [nc.dram_tensor(f"partition_column_{x}", (2, EDGES), BF16, kind="Internal").ap() for x in ("src", "dst")]
        near_d = nc.dram_tensor("near", (1, EDGES), BF16, kind="Internal").ap()

        ident = sb("ident", [P, P])
        upper = sb("upper", [P, P])
        identb = sb("identb", [P, P], BF16)
        iota2 = sb("iota2", [P, 2])
        iotaw = sb("iotaw", [P, 2 * P])
        ones = sb("ones", [P, P])
        onesb = sb("onesb", [P, P], BF16)
        strides = sb("strides", [2, P], BF16)
        w0d, wld, wf1d, wf2d, w1d, w2d, w3d = (sb(f"{x}d", [P, P]) for x in ("w0", "wl", "wf1", "wf2", "w1", "w2", "w3"))
        bf1d, b1d = sb("bf1d", [P, 1]), sb("b1d", [P, 1])
        SUMMED = ("bf2", "bl", "b2")
        bias_r = sb("bias_rest", [1, 1 + PARTS, len(SUMMED), D])
        bias_p = sb("bias_parts", [1, PARTS, len(SUMMED), D], BF16)
        bias_b = sb("bias_b", [PARTS, len(SUMMED), D], BF16)
        bf2b, blb, b2b = (bias_b[:, i, :] for i in range(len(SUMMED)))
        flag = sb("flag", [1, 2], I32)
        base = sb("base", [1, TURNS], I32)
        trash = sb("trash", [P, 1])
        zeros = sb("zeros", [P, ZR * (D + 1)])
        gamma = sb("gamma", [P, D])
        beta = sb("beta", [P, D])
        bias3 = sb("bias3", [P, D])

        xr = sb("x_rows", [P, NT * D])
        dinv = sb("dinv", [P, NT])

        psb = [ps(f"ps_{n}") for n in range(8)]

        settled = ctx.enter_context(nc.semaphore("settled"))
        s_const = counter("s_const")
        s_load = counter("s_load")
        s_zero = counter("s_zero")
        s_diag = counter("s_diag")

        def settle(eng):
            eng.sem_inc(settled, 1)

        loads = [(bias_r[:, 0, i, :], a[name]) for i, name in enumerate(SUMMED)] + [
            (gamma[:, :], a["gamma"].to_broadcast([P, D])), (beta[:, :], a["beta"].to_broadcast([P, D])),
            (bias3[:, :], a["bias3"].to_broadcast([P, D])),
            (xr[:, :], a["x"])]
        weights = ((w0d, "L0_gnn_W"), (wld, "WlT"), (wf1d, "Wf1T"), (wf2d, "Wf2T"), (w1d, "L2_gnn_W1"),
                   (w2d, "L2_gnn_W2"), (w3d, "L3_gnn_weight"))
        blocks = [(w[u * D:(u + 1) * D, u * D:(u + 1) * D], a[name]) for w, name in weights for u in range(2)] + [
            (w[u * D:(u + 1) * D, :], a[name]) for w, name in ((bf1d, "bf1"), (b1d, "b1")) for u in range(2)]

        with nc.Block() as block:
            @block.sync
            def _(sp):
                for dst, src in loads:
                    sp.dma_start(dst, src).then_inc(s_load.sem, 16)
                sp.wait_ge(s_zero.sem, len(weights))
                for dst, src in blocks:
                    sp.dma_start(dst, src).then_inc(s_diag.sem, 16)
                sp.wait_ge(s_zero.sem, len(weights) + 2 * PARTS)
                for m in range(PARTS):
                    sp.dma_start(bias_b[m:m + 1, :, :], bias_p[:, m, :, :]).then_inc(s_diag.sem, 16)
                sp.wait_ge(s_load.sem, 16 * len(loads))
                sp.wait_ge(s_diag.sem, 16 * (len(blocks) + PARTS))

            @block.gpsimd
            def _(pool):
                pool.memset(ident[:, :], 0.0).then_inc(s_const.sem, 1)
                pool.memset(upper[:, :], 1.0).then_inc(s_const.sem, 1)
                pool.memset(zeros[:, :], 0.0).then_inc(s_const.sem, 1)
                pool.memset(ones[:, :], 1.0).then_inc(s_const.sem, 1)
                pool.memset(onesb[:, :], 1.0).then_inc(s_const.sem, 1)
                pool.iota(iota2[:, :], pattern=[[P, 2]], base=0, channel_multiplier=1,
                          allow_small_or_imprecise_dtypes=True).then_inc(s_const.sem, 1)
                pool.iota(iotaw[:, :], pattern=[[1, 2 * P]], base=0, channel_multiplier=0,
                          allow_small_or_imprecise_dtypes=True).then_inc(s_const.sem, 1)
                pool.iota(trash[:, :], pattern=[[0, 1]], base=ROWS, channel_multiplier=1,
                          allow_small_or_imprecise_dtypes=True).then_inc(s_const.sem, 1)
                pool.memset(strides[:, :], 1.0).then_inc(s_const.sem, 1)
                pool.wait_ge(s_const.sem, 9)
                pool.memset(strides[0:1, :], float(NT)).then_inc(s_const.sem, 1)
                pool.affine_select(out=ident[:, :], in_=ident[:, :], compare_op=ALU.not_equal, fill=1.0,
                                   base=0, pattern=[[-1, P]], channel_multiplier=1).then_inc(s_const.sem, 1)
                pool.affine_select(out=upper[:, :], in_=upper[:, :], compare_op=ALU.is_ge, fill=0.0,
                                   base=0, pattern=[[1, P]], channel_multiplier=-1).then_inc(s_const.sem, 1)
                pool.wait_ge(s_const.sem, 12)
                pool.tensor_copy(identb[:, :], ident[:, :]).then_inc(s_const.sem, 1)
                pool.wait_ge(s_const.sem, 13)

            @block.vector
            def _(dve):
                for w, _name in weights:
                    dve.memset(w[:, :], 0.0).then_inc(s_zero.sem, 1)
                dve.wait_ge(s_load.sem, 16 * len(loads))
                for m in range(PARTS):
                    n = len(weights) + 2 * m
                    rest, piece = bias_r[:, m, :, :], bias_p[:, m, :, :]
                    dve.tensor_copy(piece, rest).then_inc(s_zero.sem, 1)
                    dve.wait_ge(s_zero.sem, n + 1)
                    dve.tensor_tensor(bias_r[:, m + 1, :, :], rest, piece, ALU.subtract).then_inc(s_zero.sem, 1)
                    dve.wait_ge(s_zero.sem, n + 2)

        turns = "o (r e) -> r (o e)"

        def index_stage():
            ictx = ExitStack()
            with ictx:
                def sbi(name, shape, dt=F32):
                    return ictx.enter_context(nc.sbuf_tensor(name, shape, dt))
                src, dst, hi, lo, row = (sbi(name, [P, TILES], I32) for name in ("src_raw", "dst_raw", "hi", "lo", "row"))
                rowf, nearf = sbi("rowf", [P, TILES]), sbi("near_f", [P, TILES])
                srct, dstt, hit, lot = (sbi(name, [TURNS, GROUP * P], I32) for name in ("srct", "dstt", "hit", "lot"))
                neart, hib, lob = (sbi(name, [TURNS, GROUP * P], BF16) for name in ("neart", "hib", "lob"))
                columnt = sbi("columnt", [TURNS, 1], I32)
                baset = sbi("baset", [TURNS, 1])
                basef = sbi("basef", [1, TURNS])
                lim = sbi("lim", [P, 4])
                i_in = [ictx.enter_context(nc.semaphore(f"i_in_{x}")) for x in ("dst", "src", "srct", "dstt")]
                i_out, i_dve, i_act, i_pe = (ictx.enter_context(nc.semaphore(x)) for x in ("i_out", "i_dve", "i_act", "i_pe"))
                marks = {}
                with nc.Block() as block:
                    @block.vector
                    def _(dve):
                        n = [0]

                        def step(i, name=None):
                            i.then_inc(i_dve, 1)
                            n[0] += 1
                            dve.wait_ge(i_dve, n[0])
                            if name:
                                marks[name] = n[0]
                        dve.wait_ge(i_in[0], 16)
                        first = dst[0:1, :].rearrange("p (r j) -> p r j", j=GROUP)[:, :, 0]
                        step(dve.tensor_scalar(base[:, :], first, SHIFT, None, ALU.logical_shift_right))
                        step(dve.tensor_copy(basef[:, :], base[:, :]), "basef")
                        dve.wait_ge(i_in[1], 16)
                        step(dve.tensor_scalar(hi[:, :], src[:, :], SHIFT, None, ALU.logical_shift_right))
                        step(dve.tensor_scalar(lo[:, :], src[:, :], P - 1, None, ALU.bitwise_and))
                        step(dve.scalar_tensor_tensor(out=row[:, :], in0=lo[:, :], scalar=float(NT), in1=hi[:, :],
                                                      op0=ALU.mult, op1=ALU.add), "row")
                        dve.wait_ge(i_in[2], 16)
                        step(dve.tensor_scalar(hit[:, :], srct[:, :], SHIFT, None, ALU.logical_shift_right), "hit")
                        step(dve.tensor_scalar(lot[:, :], srct[:, :], P - 1, None, ALU.bitwise_and), "lot")
                        dve.wait_ge(i_in[3], 16)
                        step(dve.tensor_scalar(columnt[:, :], dstt[:, 0:1], SHIFT, None, ALU.logical_shift_right))
                        step(dve.tensor_scalar(baset[:, :], columnt[:, :], float(P), None, ALU.mult))
                        step(dve.tensor_scalar(neart[:, :], dstt[:, :], baset[:, 0:1], None, ALU.subtract), "neart")
                        dve.wait_ge(i_pe, 1)
                        bb = psb[0][:, 0:TURNS].unsqueeze(2).to_broadcast([P, TURNS, GROUP])
                        view = [v.rearrange("p (r j) -> p r j", j=GROUP) for v in (nearf[:, :], dst[:, :])]
                        step(dve.scalar_tensor_tensor(out=view[0], in0=bb, scalar=-float(P), in1=view[1],
                                                      op0=ALU.mult, op1=ALU.add), "nearf")
                        step(dve.tensor_reduce(lim[:, 0:1], nearf[:, :], AX.X, ALU.min))
                        step(dve.tensor_reduce(lim[:, 1:2], nearf[:, :], AX.X, ALU.max))
                        step(dve.tensor_scalar(lim[:, 2:3], lim[:, 0:1], -0.5, None, ALU.is_lt))
                        step(dve.scalar_tensor_tensor(out=lim[:, 3:4], in0=lim[:, 1:2], scalar=2 * P - 0.5, in1=lim[:, 2:3],
                                                      op0=ALU.is_gt, op1=ALU.add), "outside")
                        dve.wait_ge(i_pe, 2)
                        step(dve.tensor_scalar(flag[:, 0:1], psb[1][0:1, 0:1], 0.5, None, ALU.is_lt))
                        step(dve.tensor_scalar(flag[:, 1:2], psb[1][0:1, 0:1], 0.5, None, ALU.is_gt))

                    @block.scalar
                    def _(act):
                        act.wait_ge(i_dve, marks["row"])
                        act.activation(rowf[:, :], row[:, :], ACT.Copy).then_inc(i_act, 1)
                        act.wait_ge(i_dve, marks["hit"])
                        act.activation(hib[:, :], hit[:, :], ACT.Copy).then_inc(i_act, 1)
                        act.wait_ge(i_dve, marks["lot"])
                        act.activation(lob[:, :], lot[:, :], ACT.Copy).then_inc(i_act, 1)

                    @block.tensor
                    def _(pe):
                        pe.wait_ge(i_dve, marks["basef"])
                        pe.matmul(psb[0][:, 0:TURNS], ones[0:1, :], basef[:, :], start=True, stop=True).then_inc(i_pe, 1)
                        pe.wait_ge(i_dve, marks["outside"])
                        pe.matmul(psb[1][0:1, 0:1], lim[:, 3:4], ones[:, 0:1], start=True, stop=True).then_inc(i_pe, 1)

                    @block.sync
                    def _(sp):
                        for k, (to, name) in enumerate(((dst, "dstT"), (src, "srcT"), (srct, "src"), (dstt, "dst"))):
                            sp.dma_start(to[:, :], a[name]).then_inc(i_in[k], 16)
                        stores = ((i_dve, marks["row"], row_d[0], row), (i_act, 1, rowf_d[0], rowf),
                                  (i_dve, marks["neart"], near_d.rearrange(turns, r=TURNS), neart),
                                  (i_act, 2, hl_d[0][1:2, :].rearrange(turns, r=TURNS), hib),
                                  (i_act, 3, hl_d[0][0:1, :].rearrange(turns, r=TURNS), lob),
                                  (i_dve, marks["nearf"], nearf_d, nearf))
                        for sem, at, to, made in stores:
                            sp.wait_ge(sem, at)
                            sp.dma_start(to, made[:, :]).then_inc(i_out, 16)
                        sp.wait_ge(i_out, 16 * len(stores))

        def far_index_stage():
            ictx = ExitStack()
            with ictx:
                def sbi(name, shape, dt=F32):
                    return ictx.enter_context(nc.sbuf_tensor(name, shape, dt))
                dst, hi, lo = (sbi(f"far_{name}", [P, TILES], I32) for name in ("dst", "hi", "lo"))
                rowf = sbi("far_rowf", [P, TILES])
                dstt, hit, lot = (sbi(f"far_{name}", [TURNS, GROUP * P], I32) for name in ("dstt", "hit", "lot"))
                hib, lob = (sbi(f"far_{name}", [TURNS, GROUP * P], BF16) for name in ("hib", "lob"))
                x_in, x_out, x_dve = (ictx.enter_context(nc.semaphore(x)) for x in ("x_in", "x_out", "x_dve"))
                with nc.Block() as block:
                    @block.vector
                    def _(dve):
                        with under(dve, 1):
                            dve.wait_ge(x_in, 32)
                            makes = (lambda: dve.tensor_scalar(hi[:, :], dst[:, :], SHIFT, None, ALU.logical_shift_right),
                                     lambda: dve.tensor_scalar(lo[:, :], dst[:, :], P - 1, None, ALU.bitwise_and),
                                     lambda: dve.scalar_tensor_tensor(out=dst[:, :], in0=lo[:, :], scalar=float(NT),
                                                                      in1=hi[:, :], op0=ALU.mult, op1=ALU.add),
                                     lambda: dve.tensor_copy(rowf[:, :], dst[:, :]),
                                     lambda: dve.tensor_scalar(hit[:, :], dstt[:, :], SHIFT, None, ALU.logical_shift_right),
                                     lambda: dve.tensor_scalar(lot[:, :], dstt[:, :], P - 1, None, ALU.bitwise_and),
                                     lambda: dve.tensor_copy(hib[:, :], hit[:, :]),
                                     lambda: dve.tensor_copy(lob[:, :], lot[:, :]))
                            for k, make in enumerate(makes):
                                make().then_inc(x_dve, 1)
                                dve.wait_ge(x_dve, k + 1)

                    @block.sync
                    def _(sp):
                        with under(sp, 1):
                            sp.dma_start(dst[:, :], a["dstT"]).then_inc(x_in, 16)
                            sp.dma_start(dstt[:, :], a["dst"]).then_inc(x_in, 16)
                            sp.wait_ge(x_dve, 8)
                            sp.dma_start(row_d[1], dst[:, :]).then_inc(x_out, 16)
                            sp.dma_start(rowf_d[1], rowf[:, :]).then_inc(x_out, 16)
                            sp.dma_start(hl_d[1][0:1, :].rearrange(turns, r=TURNS), lob[:, :]).then_inc(x_out, 16)
                            sp.dma_start(hl_d[1][1:2, :].rearrange(turns, r=TURNS), hib[:, :]).then_inc(x_out, 16)
                            sp.wait_ge(x_out, 64)

        def under(eng, which):
            return eng.If(eng.value_load(flag[0:1, which:which + 1], min_val=0, max_val=1))

        index_stage()
        far_index_stage()
        tab3 = sb("tab3", [P, NT, PARTS, D], BF16)
        acc = sb("acc", [P, NT, D])

        def fill_piece(n, k, q):
            W, rows = width[n], PROWS // P
            lo, hi = q * ZR, min((q + 1) * ZR, rows)
            return part[n][k].rearrange("(p a) w -> p (a w)", p=P)[:, lo * W:hi * W], (hi - lo) * W

        def half_of(c):
            return 0 if c * CHUNK < HALVES[0][1] else 1

        def wait(eng, cnt_, r, n_, per=CHUNKS, credit=CREDIT):
            eng.wait_ge(cnt_.sem, r * per + (cnt_.at(credit + n_)))

        def dma_wait(eng, cnt_, r, m=1):
            eng.wait_ge(cnt_.sem, r * (16 * m) + cnt_.at(16 * m))

        def cols(src, r, h, m=1):
            lo, hi = HALVES[h]
            return src[:, bass.ds(r * (GROUP * m) + lo * m, (hi - lo) * m)]

        def spread_rows(pe, hl, c):
            lo, hi = c * CHUNK * P, (c + 1) * CHUNK * P
            pe.matmul(psb[0][:, :], strides[:, :], hl[:, lo:lo + 4 * P], start=True, stop=True)
            return pe.matmul(psb[1][:, 0:P], strides[:, :], hl[:, lo + 4 * P:hi], start=True, stop=True)

        PAIRS = CHUNK // 2

        def filter_buffers(make):
            return (make("ea2", [P, CHUNKS, PAIRS * P]), make("ea1", [D, CHUNKS, P]), make("hT", [P, (PAIRS + 1) * P]))

        def load_attributes(sp, ea2, ea1, r, h, count):
            lo, hi = HALVES[h][0] // CHUNK, HALVES[h][1] // CHUNK
            for buf, src, m in ((ea2, a["ea2"], PAIRS * P), (ea1, a["ea1"], P)):
                sp.dma_start(buf[:, lo:hi, :].rearrange("p c e -> p (c e)"),
                             src[:, bass.ds(r * (CHUNKS * m) + lo * m, (hi - lo) * m)]).then_inc(count.sem, 16)

        def filter_first(pe, f1, ea2, ea1, c):
            pe.matmul(f1[:, 0:PAIRS * P], wf1d[:, :], ea2[:, c, :], start=True, stop=True)
            return pe.matmul(f1[0:D, PAIRS * P:(PAIRS + 1) * P], wf1d[0:D, 0:D], ea1[:, c, :], start=True, stop=True)

        def filter_silu(act, f1, hT):
            act.activation(hT[:, 0:PAIRS * P], f1[:, 0:PAIRS * P], ACT.Silu, bias=bf1d[:, 0:1])
            rest = slice(PAIRS * P, (PAIRS + 1) * P)
            return act.activation(hT[0:D, rest], f1[0:D, rest], ACT.Silu, bias=bf1d[0:D, 0:1])

        def filter_second(pe, f2, hT):
            pe.matmul(f2, onesb[0:PARTS, :], bf2b[:, :].unsqueeze(1).to_broadcast([PARTS, CHUNK, D]), start=True, stop=False)
            for q in range(PAIRS):
                pe.matmul(f2[:, 2 * q * D:2 * (q + 1) * D], hT[:, q * P:(q + 1) * P], wf2d[:, :], start=False, stop=False)
            return pe.matmul(f2[:, 2 * PAIRS * D:CHUNK * D], hT[0:D, PAIRS * P:(PAIRS + 1) * P], wf2d[0:D, 0:D],
                             start=False, stop=True)

        s_tabd = counter("tab_in_dram")
        s_rows = counter("rows_whole")

        sem_gidx = [counter(f"gidx_in_{h}") for h in range(2)]
        sem_sidx = [counter(f"sidx_in_{h}") for h in range(2)]
        sem_ew = [counter(f"ew_in_{h}") for h in range(2)]
        sem_ea = [counter(f"ea_in_{h}") for h in range(2)]
        sem_gath = [counter(f"gathered_{j}") for j in range(GROUP)]
        sem_tab = [counter(f"added_{k}") for k in range(TABLES)]
        sem_hl = [counter(f"hl_in_{h}") for h in range(2)]
        s_bc = counter("bcast_done")
        s_sel = counter("sel_done")
        s_tr = counter("trash_done")
        s_fin = counter("fin_done")
        s_msg = counter("msg_done")
        s_f1 = counter("f1_done")
        s_h = counter("silu_done")
        s_f2 = counter("f2_done")
        s_mg = counter("merge_done")
        s_out = counter("out_done")

        def far_pass(n, gx, sx, ew_d=None, filtered=False):
            W = width[n]
            made = ew_d is not None or filtered
            ectx = ExitStack()
            with ectx:
                def sbe(name, shape, dt=F32):
                    return ectx.enter_context(nc.sbuf_tensor(f"{name}_{n}", shape, dt))

                gidx = sbe("gidx", [P, GROUP], I32)
                idxf = sbe("idxf", [P, GROUP])
                hl = sbe("hl", [2, GROUP * P], BF16)
                cnt = sbe("cnt", [P, GROUP])
                off = sbe("off", [P, GROUP])
                fin = sbe("fin", [P, GROUP], I32)
                ew = sbe("ew", [P, GROUP])
                g = sbe("g", [P, GROUP, D])
                msg = sbe("msg", [P, GROUP, W]) if made else g
                sel = sbe("sel", [P, GROUP, P])
                o = sbe("o", [P, GROUP, W])
                ea2, ea1, hT = filter_buffers(sbe) if filtered else (None, None, None)

                def bc(k):
                    return psb[k // 4][:, (k % 4) * P:(k % 4 + 1) * P]

                merged = psb[2][:, 0:CHUNK * W]
                f2 = psb[3][:, 0:CHUNK * D]
                f1 = psb[4]

                def load_half(sp, h, r):
                    lo, hi = HALVES[h]

                    def cols(src, m=1):
                        return src[:, bass.ds(r * (GROUP * m) + lo * m, (hi - lo) * m)]
                    sp.dma_start(gidx[:, lo:hi], cols(row_d[gx])).then_inc(sem_gidx[h].sem, 16)
                    sp.dma_start(idxf[:, lo:hi], cols(rowf_d[sx])).then_inc(sem_sidx[h].sem, 16)
                    sp.dma_start(hl[:, lo * P:hi * P], cols(hl_d[sx], P)).then_inc(sem_hl[h].sem, 16)
                    if ew_d is not None:
                        sp.dma_start(ew[:, lo:hi], cols(ew_d)).then_inc(sem_ew[h].sem, 16)
                    if filtered:
                        load_attributes(sp, ea2, ea1, r, h, sem_ea[h])

                def half_of(c):
                    return 0 if c * CHUNK < HALVES[0][1] else 1

                def tables_free(eng, r, c):
                    for k in range(TABLES):
                        eng.wait_ge(sem_tab[k].sem, sem_tab[k].at(16 * (CREDIT * r + c + 1)) if isinstance(r, int)
                                    else r * (16 * CREDIT) + sem_tab[k].at(16 * (c + 1)))

                def wait(eng, cnt_, r, n_, per=CHUNKS, credit=CREDIT):
                    eng.wait_ge(cnt_.sem, r * per + (cnt_.at(credit + n_)))

                with nc.Block() as block:
                    @block.sync
                    def _(sp):
                        with under(sp, 1):
                          if n in (1, 3):
                              sp.wait_ge(s_rows.sem, s_rows.at(2))
                              sp.dma_start(table[n].rearrange("(p t) d -> p (t d)", p=P), acc[:, :, :].rearrange("p t d -> p (t d)"))\
                                  .then_inc(s_tabd.sem, 16)
                          for h in range(2):
                              load_half(sp, h, 0)

                          def body(r):
                              for h in range(2):
                                  wait(sp, s_mg, r, HALVES[h][1] // CHUNK)
                                  settle(sp)
                                  wait(sp, s_fin, r, HALVES[h][1] // CHUNK)
                                  settle(sp)
                                  load_half(sp, h, r + 1)
                          with sp.Fori(0, TURNS - 1) as r:
                              body(r)

                    @block.gpsimd
                    def _(pool):
                        with under(pool, 1):
                          def gather(j, r):
                              c = j // CHUNK
                              h = half_of(c)
                              if j % CHUNK == 0:
                                  pool.wait_ge(sem_gidx[h].sem, r * 16 + sem_gidx[h].at(16))
                                  wait(pool, s_mg, r, c + 1 - CHUNKS)
                                  settle(pool)
                              pool.indirect_dma_start(
                                  out=g[:, j, :], out_offset=None, in_=table[n],
                                  in_offset=bass.IndirectOffsetOnAxis(ap=gidx[:, j:j + 1], axis=0))\
                                  .then_inc(sem_gath[j].sem, 16)

                          def scatter(j, r):
                              c, k = divmod(j, CHUNK)
                              if k == 0:
                                  wait(pool, s_out, r, c + 1)
                                  wait(pool, s_fin, r, c + 1)
                              pool.wait_ge(sem_tab[k].sem, r * (16 * CHUNKS) + sem_tab[k].at(16 * (CREDIT + c)))
                              settle(pool)
                              pool.indirect_dma_start(
                                  out=part[n][k], out_offset=bass.IndirectOffsetOnAxis(ap=fin[:, j:j + 1], axis=0),
                                  in_=o[:, j, :], in_offset=None, compute_op=ALU.add)\
                                  .then_inc(sem_tab[k].sem, 16)

                          for q in range(CREDIT):
                              for k in range(TABLES):
                                  if q:
                                      pool.wait_ge(sem_tab[k].sem, sem_tab[k].at(16 * q))
                                  dst, m = fill_piece(n, k, q)
                                  pool.dma_start(dst, zeros[:, 0:m]).then_inc(sem_tab[k].sem, 16)
                          if n in (1, 3):
                              pool.wait_ge(s_tabd.sem, s_tabd.at(16))
                          for h in range(2):
                              pool.wait_ge(sem_gidx[h].sem, sem_gidx[h].at(16))
                          for j in range(AHEAD):
                              pool.indirect_dma_start(
                                  out=g[:, j, :], out_offset=None, in_=table[n],
                                  in_offset=bass.IndirectOffsetOnAxis(ap=gidx[:, j:j + 1], axis=0))\
                                  .then_inc(sem_gath[j].sem, 16)

                          def body(r, last):
                              for j in range(GROUP):
                                  ahead = j + AHEAD
                                  if ahead < GROUP:
                                      gather(ahead, r)
                                  elif not last:
                                      gather(ahead - GROUP, r + 1)
                                  scatter(j, r)
                          with pool.Fori(0, TURNS - 1) as r:
                              body(r, False)
                          body(TURNS - 1, True)
                          settle(pool)
                          for k in range(TABLES):
                              pool.wait_ge(sem_tab[k].sem, sem_tab[k].at(16 * CHUNKS * (TURNS + 1)))

                    @block.vector
                    def _(dve):
                        with under(dve, 1):
                          if n in (1, 3):
                              dve.tensor_tensor(acc[:, :, :], tab3[:, :, 0, :], tab3[:, :, 1, :], ALU.add).then_inc(s_rows.sem, 1)
                              dve.wait_ge(s_rows.sem, s_rows.at(1))
                              dve.tensor_tensor(acc[:, :, :], acc[:, :, :], tab3[:, :, 2, :], ALU.add).then_inc(s_rows.sem, 1)
                          for s in (s_sel, s_tr, s_fin, s_msg):
                              dve.sem_inc(s.sem, CREDIT)
                          if filtered:
                              dve.memset(msg[:, :, D:D + 1], 1.0).then_inc(s_h.sem, 1)

                          def body(r):
                              for c in range(CHUNKS):
                                  lo, hi = c * CHUNK, (c + 1) * CHUNK
                                  h = half_of(c)
                                  if lo == HALVES[h][0]:
                                      dve.wait_ge(sem_sidx[h].sem, r * 16 + sem_sidx[h].at(16))
                                  wait(dve, s_bc, r, c + 1)
                                  wait(dve, s_mg, r, c + 1 - CHUNKS)
                                  wait(dve, s_tr, r, c + 1 - CHUNKS)
                                  settle(dve)
                                  for j in range(lo, hi):
                                      i = dve.scalar_tensor_tensor(
                                          out=sel[:, j, :], in0=bc(j - lo), scalar=idxf[:, j:j + 1], in1=upper[:, :],
                                          op0=ALU.is_equal, op1=ALU.mult, accum_out=cnt[:, j:j + 1])
                                  i.then_inc(s_sel.sem, 1)
                                  wait(dve, s_sel, r, c + 1)
                                  wait(dve, s_fin, r, c + 1 - CHUNKS)
                                  settle(dve)
                                  dve.tensor_scalar(off[:, lo:hi], cnt[:, lo:hi], 1.5, trash[:, 0:1], ALU.is_gt, ALU.mult)\
                                      .then_inc(s_tr.sem, 1)
                                  wait(dve, s_tr, r, c + 1)
                                  tables_free(dve, r, c)
                                  settle(dve)
                                  dve.tensor_tensor(fin[:, lo:hi], off[:, lo:hi], idxf[:, lo:hi], ALU.max)\
                                      .then_inc(s_fin.sem, 1)
                                  if not made:
                                      continue
                                  for j in range(lo, hi):
                                      dve.wait_ge(sem_gath[j].sem, r * 16 + sem_gath[j].at(16))
                                  if ew_d is not None:
                                      dve.wait_ge(sem_ew[h].sem, r * 16 + sem_ew[h].at(16))
                                      wait(dve, s_mg, r, c + 1 - CHUNKS)
                                      settle(dve)
                                      dve.tensor_tensor(msg[:, lo:hi, :], g[:, lo:hi, :],
                                                        ew[:, lo:hi].unsqueeze(2).to_broadcast([P, CHUNK, D]), ALU.mult)\
                                          .then_inc(s_msg.sem, 1)
                                  else:
                                      wait(dve, s_f2, r, c + 1)
                                      settle(dve)
                                      dve.tensor_tensor(msg[:, lo:hi, 0:D], g[:, lo:hi, :],
                                                        f2.rearrange("p (k d) -> p k d", d=D), ALU.mult)\
                                          .then_inc(s_msg.sem, 1)
                          with dve.Fori(0, TURNS) as r:
                              body(r)

                    @block.tensor
                    def _(pe):
                        with under(pe, 1):
                          for s in (s_bc, s_f1, s_f2, s_mg):
                              pe.sem_inc(s.sem, CREDIT)

                          def body(r):
                              for c in range(CHUNKS):
                                  lo, hi = c * CHUNK, (c + 1) * CHUNK
                                  h = half_of(c)
                                  if lo == HALVES[h][0]:
                                      pe.wait_ge(sem_hl[h].sem, r * 16 + sem_hl[h].at(16))
                                  wait(pe, s_sel, r, c)
                                  settle(pe)
                                  spread_rows(pe, hl, c).then_inc(s_bc.sem, 1)
                                  if filtered:
                                      dma_wait(pe, sem_ea[h], r, 2)
                                      wait(pe, s_h, r, c)
                                      settle(pe)
                                      filter_first(pe, f1, ea2, ea1, c).then_inc(s_f1.sem, 1)
                                      wait(pe, s_h, r, c + 1)
                                      wait(pe, s_msg, r, c)
                                      settle(pe)
                                      filter_second(pe, f2, hT).then_inc(s_f2.sem, 1)
                                  wait(pe, s_sel, r, c + 1)
                                  wait(pe, s_out, r, c)
                                  if made:
                                      wait(pe, s_msg, r, c + 1)
                                  else:
                                      for j in range(lo, hi):
                                          pe.wait_ge(sem_gath[j].sem, r * 16 + sem_gath[j].at(16))
                                  settle(pe)
                                  for j in range(lo, hi):
                                      k = j - lo
                                      i = pe.matmul(merged[:, k * W:(k + 1) * W], sel[:, j, :], msg[:, j, :],
                                                    start=True, stop=True)
                                  i.then_inc(s_mg.sem, 1)
                          with pe.Fori(0, TURNS) as r:
                              body(r)

                    @block.scalar
                    def _(act):
                        with under(act, 1):
                          act.sem_inc(s_out.sem, CREDIT)
                          if filtered:
                              act.sem_inc(s_h.sem, CREDIT - 1)

                          def body(r):
                              for c in range(CHUNKS):
                                  lo, hi = c * CHUNK, (c + 1) * CHUNK
                                  if filtered:
                                      wait(act, s_f1, r, c + 1)
                                      wait(act, s_f2, r, c)
                                      settle(act)
                                      filter_silu(act, f1, hT).then_inc(s_h.sem, 1)
                                  wait(act, s_mg, r, c + 1)
                                  tables_free(act, r, c)
                                  settle(act)
                                  act.activation(o[:, lo:hi, :], merged.rearrange("p (k w) -> p k w", w=W), ACT.Copy)\
                                      .then_inc(s_out.sem, 1)
                          with act.Fori(0, TURNS) as r:
                              body(r)

            for c_ in sem_gidx + sem_sidx + sem_hl + sem_gath:
                c_.base += 16 * TURNS
            if ew_d is not None:
                for c_ in sem_ew:
                    c_.base += 16 * TURNS
            if filtered:
                for c_ in sem_ea:
                    c_.base += 32 * TURNS
                for c_ in (s_f1, s_h, s_f2):
                    c_.base += CHUNKS * TURNS + CREDIT
            else:
                for c_ in (s_f1, s_f2):
                    c_.base += CREDIT
            for c_ in sem_tab:
                c_.base += 16 * CHUNKS * (TURNS + 1)
            if n in (1, 3):
                s_tabd.base += 16
                s_rows.base += 2
            for c_ in (s_sel, s_tr, s_fin, s_bc, s_mg, s_out):
                c_.base += CHUNKS * TURNS + CREDIT
            s_msg.base += (CHUNKS * TURNS if made else 0) + CREDIT

        def far_collect(n):
            cctx = ExitStack()
            with cctx:
                pin = [cctx.enter_context(nc.sbuf_tensor(f"fpin{k}_{n}", [P, NCH, D], F32)) for k in range(TABLES)]
                with nc.Block() as block:
                    @block.sync
                    def _(sp):
                        with under(sp, 1):
                            for q in range(NT // NCH):
                                if q:
                                    sp.wait_ge(f_sum.sem, f_sum.at(4 * q))
                                for k in range(TABLES):
                                    sp.dma_start(pin[k][:, :, :].rearrange("p a w -> p (a w)"),
                                                 part[n][k][0:ROWS, :].rearrange("(p a) w -> p (a w)", p=P)
                                                 [:, q * NCH * D:(q + 1) * NCH * D]).then_inc(f_part[k].sem, 16)

                    @block.vector
                    def _(dve):
                        with under(dve, 1):
                            for q in range(NT // NCH):
                                dst = acc[:, q * NCH:(q + 1) * NCH, :]
                                for k in range(TABLES):
                                    dve.wait_ge(f_part[k].sem, f_part[k].at(16 * (q + 1)))
                                for k in range(1, TABLES):
                                    dve.tensor_tensor(dst, pin[0][:, :, :] if k == 1 else dst, pin[k][:, :, :], ALU.add)\
                                        .then_inc(f_sum.sem, 1)
                                    dve.wait_ge(f_sum.sem, f_sum.at(4 * q + k))
            for c_ in f_part:
                c_.base += 16 * (NT // NCH)
            f_sum.base += 4 * (NT // NCH)

        f_part = [counter(f"far_part_{k}") for k in range(TABLES)]
        f_sum = counter("far_sum")

        m_gidx = [counter(f"m_gidx_in_{h}") for h in range(2)]
        m_near = [counter(f"m_near_in_{h}") for h in range(2)]
        m_ew = [counter(f"m_ew_in_{h}") for h in range(2)]
        m_ea = [counter(f"m_ea_in_{h}") for h in range(2)]
        m_rowf = [counter(f"m_rowf_in_{h}") for h in range(2)]
        m_hl = [counter(f"m_hl_in_{h}") for h in range(2)]
        m_gath = [counter(f"m_gathered_{j}") for j in range(GROUP)]
        m_tab = [counter(f"m_added_{k}") for k in range(TABLES)]
        m_fill = counter("m_filled")
        m_land = counter("m_landed")
        m_bc = counter("m_bcast_done")
        m_m = counter("m_product_done")
        m_hi = counter("m_hi_done")
        m_r = counter("m_rest_done")
        m_mid = counter("m_mid_done")
        m_sel = counter("m_sel_done")
        m_tr = counter("m_trash_done")
        m_fin = counter("m_fin_done")
        m_msg = counter("m_msg_done")
        m_f1 = counter("m_f1_done")
        m_h = counter("m_silu_done")
        m_f2 = counter("m_f2_done")
        m_ex = counter("m_read_done")
        m_g = counter("m_copy_done")
        m_mg = counter("m_merge_done")
        m_out = counter("m_out_done")
        m_acc = counter("m_acc_done")

        def near_sum_pass(n, ew_d=None):
            ectx = ExitStack()
            with ectx:
                def sbe(name, shape, dt=F32):
                    return ectx.enter_context(nc.sbuf_tensor(f"m_{name}_{n}", shape, dt))
                gidx = sbe("gidx", [P, GROUP], I32)
                near = sbe("near", [P, GROUP])
                ew = sbe("ew", [P, GROUP])
                g = sbe("g", [P, GROUP, D])
                msg = sbe("msg", [P, GROUP, D]) if ew_d is not None else g
                hot = sbe("hot", [P, GROUP, 2 * P])
                psS = [psb[0][:, 0:D], psb[1][:, 0:D]]

                with nc.Block() as block:
                    @block.sync
                    def _(sp):
                        def load(r, h):
                            lo, hi = HALVES[h]
                            sp.dma_start(gidx[:, lo:hi], cols(row_d[0], r, h)).then_inc(m_gidx[h].sem, 16)
                            sp.dma_start(near[:, lo:hi], cols(nearf_d, r, h)).then_inc(m_near[h].sem, 16)
                            if ew_d is not None:
                                sp.dma_start(ew[:, lo:hi], cols(ew_d, r, h)).then_inc(m_ew[h].sem, 16)
                        with under(sp, 0):
                            for h in range(2):
                                load(0, h)
                            for q in range(CREDIT):
                                for k in range(TABLES):
                                    dst, m = fill_piece(n + 1, k, q)
                                    sp.dma_start(dst, zeros[:, 0:m]).then_inc(m_fill.sem, 16)
                            with sp.Fori(0, TURNS - 1) as r:
                                for h in range(2):
                                    wait(sp, m_mg, r, HALVES[h][1] // CHUNK)
                                    settle(sp)
                                    load(r + 1, h)
                            sp.wait_ge(m_fill.sem, m_fill.at(16 * CREDIT * TABLES))

                    @block.gpsimd
                    def _(pool):
                        with under(pool, 0):
                            with pool.Fori(0, TURNS) as r:
                                for j in range(GROUP):
                                    c = j // CHUNK
                                    if j % CHUNK == 0:
                                        dma_wait(pool, m_gidx[half_of(c)], r)
                                        wait(pool, m_mg, r, c + 1 - CHUNKS)
                                        settle(pool)
                                    pool.indirect_dma_start(
                                        out=g[:, j, :], out_offset=None, in_=table[n],
                                        in_offset=bass.IndirectOffsetOnAxis(ap=gidx[:, j:j + 1], axis=0))\
                                        .then_inc(m_gath[j].sem, 16)

                    @block.vector
                    def _(dve):
                        with under(dve, 0):
                            for s in (m_sel, m_acc) + ((m_msg,) if ew_d is not None else ()):
                                dve.sem_inc(s.sem, CREDIT)
                            dve.memset(acc[:, :, :], 0.0).then_inc(m_acc.sem, 1)
                            with dve.Fori(0, TURNS) as r:
                                b = dve.value_load(base[0:1, bass.ds(r, 1)], min_val=0, max_val=NT - 2)
                                for c in range(CHUNKS):
                                    lo, hi = c * CHUNK, (c + 1) * CHUNK
                                    h = half_of(c)
                                    dma_wait(dve, m_near[h], r)
                                    wait(dve, m_mg, r, c + 1 - CHUNKS)
                                    settle(dve)
                                    for j in range(lo, hi):
                                        i = dve.tensor_scalar(hot[:, j, :], iotaw[:, :], near[:, j:j + 1], None, ALU.is_equal)
                                    i.then_inc(m_sel.sem, 1)
                                    if ew_d is not None:
                                        for j in range(lo, hi):
                                            dma_wait(dve, m_gath[j], r)
                                        dma_wait(dve, m_ew[h], r)
                                        settle(dve)
                                        dve.tensor_tensor(msg[:, lo:hi, :], g[:, lo:hi, :],
                                                          ew[:, lo:hi].unsqueeze(2).to_broadcast([P, CHUNK, D]), ALU.mult)\
                                            .then_inc(m_msg.sem, 1)
                                wait(dve, m_mg, r, CHUNKS)
                                dve.wait_ge(m_acc.sem, r + m_acc.at(CREDIT + 1))
                                settle(dve)
                                for m in range(2):
                                    dst = acc[:, bass.ds(b + m, 1), :].rearrange("p o d -> p (o d)")
                                    i = dve.tensor_tensor(dst, dst, psS[m], ALU.add)
                                i.then_inc(m_acc.sem, 1)
                            dve.wait_ge(m_acc.sem, m_acc.at(CREDIT + 1 + TURNS))

                    @block.tensor
                    def _(pe):
                        with under(pe, 0):
                            pe.sem_inc(m_mg.sem, CREDIT)
                            with pe.Fori(0, TURNS) as r:
                                for c in range(CHUNKS):
                                    lo, hi = c * CHUNK, (c + 1) * CHUNK
                                    if c == 0:
                                        pe.wait_ge(m_acc.sem, r + m_acc.at(CREDIT + 1))
                                    wait(pe, m_sel, r, c + 1)
                                    if ew_d is not None:
                                        wait(pe, m_msg, r, c + 1)
                                    else:
                                        for j in range(lo, hi):
                                            dma_wait(pe, m_gath[j], r)
                                    settle(pe)
                                    for j in range(lo, hi):
                                        for m in range(2):
                                            i = pe.matmul(psS[m], hot[:, j, m * P:(m + 1) * P], msg[:, j, :],
                                                          start=(j == 0), stop=(j == GROUP - 1))
                                    i.then_inc(m_mg.sem, 1)
            for c_ in m_gidx + m_near + m_gath + (m_ew if ew_d is not None else []):
                c_.base += 16 * TURNS
            m_fill.base += 16 * CREDIT * TABLES
            for c_ in [m_sel, m_mg] + ([m_msg] if ew_d is not None else []):
                c_.base += CREDIT + CHUNKS * TURNS
            m_acc.base += CREDIT + 1 + TURNS

        def near_read_pass(n, filtered=False):
            W = width[n]
            ectx = ExitStack()
            with ectx:
                def sbe(name, shape, dt=F32):
                    return ectx.enter_context(nc.sbuf_tensor(f"m_{name}_{n}", shape, dt))
                rowf = sbe("rowf", [P, GROUP])
                hl = sbe("hl", [2, GROUP * P], BF16)
                nrow = sbe("nrow", [P, GROUP, P], BF16)
                cnt = sbe("cnt", [P, GROUP])
                off = sbe("off", [P, GROUP])
                fin = sbe("fin", [P, GROUP], I32)
                part3 = sbe("part3", [P, GROUP, PARTS, W], BF16)
                g = sbe("g", [P, CHUNK, D]) if filtered else None
                m32 = sbe("m32", [P, CHUNK, D]) if filtered else None
                rest = sbe("rest", [P, CHUNK, D]) if filtered else None
                sel = sbe("sel", [P, GROUP, P], BF16)
                hot = sbe("hot", [P, GROUP, 2, P], BF16)
                o = sbe("o", [P, GROUP, W])
                ea2, ea1, hT = filter_buffers(sbe) if filtered else (None, None, None)

                def row_of(k):
                    return psb[k // 4][:, (k % 4) * P:(k % 4 + 1) * P]

                f1, f2 = psb[3], psb[4][:, 0:CHUNK * D]
                ex = psb[5][:, 0:CHUNK * D]
                ex3 = [psb[2 + k // 2][:, (k % 2) * PARTS * D:(k % 2 + 1) * PARTS * D] for k in range(CHUNK)]
                merged = psb[6][:, 0:CHUNK * W]

                with nc.Block() as block:
                    @block.sync
                    def _(sp):
                        def load(r, h):
                            lo, hi = HALVES[h]
                            sp.dma_start(hl[:, lo * P:hi * P], cols(hl_d[0], r, h, P)).then_inc(m_hl[h].sem, 16)
                            sp.dma_start(nrow[:, lo:hi, :].rearrange("p t e -> p (t e)"),
                                         cols(near_d, r, h, P).to_broadcast([P, (hi - lo) * P])).then_inc(m_near[h].sem, 16)
                            sp.dma_start(rowf[:, lo:hi], cols(rowf_d[0], r, h)).then_inc(m_rowf[h].sem, 16)
                            if filtered:
                                load_attributes(sp, ea2, ea1, r, h, m_ea[h])
                        with under(sp, 0):
                            for h in range(2):
                                load(0, h)
                            with sp.Fori(0, TURNS - 1) as r:
                                for h in range(2):
                                    wait(sp, m_fin, r, HALVES[h][1] // CHUNK)
                                    if filtered:
                                        settle(sp)
                                        wait(sp, m_f1, r, HALVES[h][1] // CHUNK)
                                    settle(sp)
                                    load(r + 1, h)

                    @block.gpsimd
                    def _(pool):
                        with under(pool, 0):
                            pool.sem_inc(m_land.sem, CREDIT - 1)
                            for k in range(TABLES):
                                pool.dma_start(part[n][k][ROWS:PROWS, :], zeros[:, 0:W]).then_inc(m_tab[k].sem, 16)
                            with pool.Fori(0, TURNS) as r:
                                for j in range(GROUP):
                                    c, k = divmod(j, CHUNK)
                                    if k == 0:
                                        wait(pool, m_out, r, c + 1)
                                        wait(pool, m_fin, r, c + 1)
                                    pool.wait_ge(m_tab[k].sem, r * (16 * CHUNKS) + m_tab[k].at(16 * (c + 1)))
                                    if k == TABLES - 1:
                                        pool.sem_inc(m_land.sem, 1)
                                    else:
                                        settle(pool)
                                    pool.indirect_dma_start(
                                        out=part[n][k], out_offset=bass.IndirectOffsetOnAxis(ap=fin[:, j:j + 1], axis=0),
                                        in_=o[:, j, :], in_offset=None, compute_op=ALU.add)\
                                        .then_inc(m_tab[k].sem, 16)
                            for k in range(TABLES):
                                pool.wait_ge(m_tab[k].sem, m_tab[k].at(16 * (CHUNKS * TURNS + 1)))

                    @block.vector
                    def _(dve):
                        def select(r, c, between):
                            lo, hi = c * CHUNK, (c + 1) * CHUNK
                            dma_wait(dve, m_rowf[half_of(c)], r)
                            dma_wait(dve, m_near[half_of(c)], r)
                            wait(dve, m_bc, r, c + 1)
                            wait(dve, m_mg, r, c + 1 - CHUNKS)
                            wait(dve, m_tr, r, c + 1 - CHUNKS)
                            settle(dve)
                            for j in range(lo, hi):
                                dve.scalar_tensor_tensor(out=sel[:, j, :], in0=row_of(j - lo), scalar=rowf[:, j:j + 1],
                                                         in1=upper[:, :], op0=ALU.is_equal, op1=ALU.mult,
                                                         accum_out=cnt[:, j:j + 1])
                            between(0)
                            for m in range(2):
                                i = dve.tensor_scalar(hot[:, lo:hi, m, :], nrow[:, lo:hi, :], iota2[:, m:m + 1], None,
                                                      ALU.is_equal)
                            i.then_inc(m_sel.sem, 1)
                            between(1)
                            wait(dve, m_sel, r, c + 1)
                            wait(dve, m_fin, r, c + 1 - CHUNKS)
                            settle(dve)
                            dve.tensor_scalar(off[:, lo:hi], cnt[:, lo:hi], 1.5, trash[:, 0:1], ALU.is_gt, ALU.mult)\
                                .then_inc(m_tr.sem, 1)
                            between(2)
                            wait(dve, m_tr, r, c + 1)
                            wait(dve, m_land, r, c + 1 - CHUNKS)
                            settle(dve)
                            dve.tensor_tensor(fin[:, lo:hi], off[:, lo:hi], rowf[:, lo:hi], ALU.max).then_inc(m_fin.sem, 1)

                        def message(r, c, stage):
                            lo, hi = c * CHUNK, (c + 1) * CHUNK
                            if not filtered:
                                return
                            if stage == 0:
                                wait(dve, m_f2, r, c + 1)
                                wait(dve, m_g, r, c + 1)
                                wait(dve, m_r, r, c)
                                settle(dve)
                                dve.tensor_tensor(m32[:, :, :], g[:, :, :], f2.rearrange("p (k d) -> p k d", d=D), ALU.mult)\
                                    .then_inc(m_m.sem, 1)
                            elif stage == 1:
                                wait(dve, m_hi, r, c + 1)
                                wait(dve, m_msg, r, c)
                                settle(dve)
                                dve.tensor_tensor(rest[:, :, :], m32[:, :, :], part3[:, lo:hi, 0, 0:D], ALU.subtract)\
                                    .then_inc(m_r.sem, 1)
                            else:
                                wait(dve, m_mid, r, c + 1)
                                settle(dve)
                                dve.tensor_tensor(part3[:, lo:hi, 2, 0:D], rest[:, :, :], part3[:, lo:hi, 1, 0:D],
                                                  ALU.subtract).then_inc(m_msg.sem, 1)

                        def body(r, last):
                            for c in range(CHUNKS):
                                def between(stage):
                                    message(r, c, stage)
                                if c + 1 < CHUNKS:
                                    select(r, c + 1, between)
                                elif not last:
                                    select(r + 1, 0, between)
                                else:
                                    for stage in range(3):
                                        between(stage)
                        with under(dve, 0):
                            for s in (m_sel, m_tr, m_fin) + ((m_m, m_r) if filtered else ()):
                                dve.sem_inc(s.sem, CREDIT)
                            if filtered:
                                dve.memset(part3[:, :, 0, D:D + 1], 1.0).then_inc(m_msg.sem, CREDIT)
                            select(0, 0, lambda stage: None)
                            with dve.Fori(0, TURNS - 1) as r:
                                body(r, False)
                            body(TURNS - 1, True)

                    @block.tensor
                    def _(pe):
                        def spread(r, c):
                            dma_wait(pe, m_hl[half_of(c)], r)
                            wait(pe, m_sel, r, c)
                            settle(pe)
                            spread_rows(pe, hl, c).then_inc(m_bc.sem, 1)

                        def merge(r, c):
                            wait(pe, m_msg if filtered else m_g, r, c + 1)
                            wait(pe, m_out, r, c)
                            settle(pe)
                            for k in range(CHUNK):
                                j = c * CHUNK + k
                                for part_ in range(PARTS):
                                    w = W if part_ == 0 else D
                                    i = pe.matmul(merged[:, k * W:k * W + w], sel[:, j, :], part3[:, j, part_, 0:w],
                                                  start=(part_ == 0), stop=(part_ == PARTS - 1))
                            i.then_inc(m_mg.sem, 1)

                        def body(r, first, last):
                            b = pe.value_load(base[0:1, bass.ds(r, 1)], min_val=0, max_val=NT - 2)
                            for c in range(CHUNKS):
                                lo, hi = c * CHUNK, (c + 1) * CHUNK
                                if c + 1 < CHUNKS:
                                    spread(r, c + 1)
                                elif not last:
                                    spread(r + 1, 0)
                                if filtered:
                                    dma_wait(pe, m_ea[half_of(c)], r, 2)
                                    wait(pe, m_h, r, c)
                                    settle(pe)
                                    filter_first(pe, f1, ea2, ea1, c).then_inc(m_f1.sem, 1)
                                wait(pe, m_sel, r, c + 1)
                                wait(pe, m_g, r, c)
                                settle(pe)
                                for k in range(CHUNK):
                                    for m in range(2):
                                        whole = tab3[:, bass.ds(b + m, 1), :, :]
                                        if not filtered:
                                            i = pe.matmul(ex3[k], hot[:, lo + k, m, :], whole.rearrange("p o s d -> p (o s d)"),
                                                          start=(m == 0), stop=(m == 1))
                                            continue
                                        for part_ in range(PARTS):
                                            i = pe.matmul(ex[:, k * D:(k + 1) * D], hot[:, lo + k, m, :],
                                                          whole[:, :, part_, :].rearrange("p o d -> p (o d)"),
                                                          start=(m == 0 and part_ == 0), stop=(m == 1 and part_ == PARTS - 1))
                                i.then_inc(m_ex.sem, 1)
                                if filtered:
                                    wait(pe, m_h, r, c + 1)
                                    wait(pe, m_m, r, c)
                                    settle(pe)
                                    filter_second(pe, f2, hT).then_inc(m_f2.sem, 1)
                                if c:
                                    merge(r, c - 1)
                                elif not first:
                                    merge(r - 1, CHUNKS - 1)
                        with under(pe, 0):
                            for s in (m_bc, m_ex, m_mg) + ((m_f1, m_f2) if filtered else ()):
                                pe.sem_inc(s.sem, CREDIT)
                            spread(0, 0)
                            body(0, True, False)
                            with pe.Fori(1, TURNS - 1) as r:
                                body(r, False, False)
                            body(TURNS - 1, False, True)
                            merge(TURNS - 1, CHUNKS - 1)

                    @block.scalar
                    def _(act):
                        def sums(r, c):
                            wait(act, m_mg, r, c + 1)
                            wait(act, m_land, r, c + 1 - CHUNKS)
                            settle(act)
                            act.activation(o[:, c * CHUNK:(c + 1) * CHUNK, :], merged.rearrange("p (k w) -> p k w", w=W),
                                           ACT.Copy).then_inc(m_out.sem, 1)

                        def body(r, first):
                            for c in range(CHUNKS):
                                lo, hi = c * CHUNK, (c + 1) * CHUNK
                                if filtered:
                                    wait(act, m_f1, r, c + 1)
                                    wait(act, m_f2, r, c)
                                    settle(act)
                                    filter_silu(act, f1, hT).then_inc(m_h.sem, 1)
                                    wait(act, m_ex, r, c + 1)
                                    wait(act, m_m, r, c)
                                    settle(act)
                                    act.activation(g[:, :, :], ex.rearrange("p (k d) -> p k d", d=D), ACT.Copy)\
                                        .then_inc(m_g.sem, 1)
                                    wait(act, m_m, r, c + 1)
                                    wait(act, m_mg, r, c + 1 - CHUNKS)
                                    settle(act)
                                    act.activation(part3[:, lo:hi, 0, 0:D], m32[:, :, :], ACT.Copy).then_inc(m_hi.sem, 1)
                                else:
                                    wait(act, m_ex, r, c + 1)
                                    wait(act, m_mg, r, c + 1 - CHUNKS)
                                    settle(act)
                                    for k in range(0, CHUNK, 2):
                                        m = min(2, CHUNK - k)
                                        i = act.activation(part3[:, lo + k:lo + k + m, :, :].rearrange("p k s d -> p (k s d)"),
                                                           psb[2 + k // 2][:, 0:m * PARTS * D], ACT.Copy)
                                    i.then_inc(m_g.sem, 1)
                                if c:
                                    sums(r, c - 1)
                                elif not first:
                                    sums(r - 1, CHUNKS - 1)
                                if filtered:
                                    wait(act, m_r, r, c + 1)
                                    settle(act)
                                    act.activation(part3[:, lo:hi, 1, 0:D], rest[:, :, :], ACT.Copy).then_inc(m_mid.sem, 1)

                        with under(act, 0):
                            for s in (m_g, m_out) + ((m_h, m_hi, m_mid) if filtered else ()):
                                act.sem_inc(s.sem, CREDIT)
                            body(0, True)
                            with act.Fori(1, TURNS) as r:
                                body(r, False)
                            sums(TURNS - 1, CHUNKS - 1)
            for c_ in m_rowf + m_hl + m_near + (m_ea * 2 if filtered else []):
                c_.base += 16 * TURNS
            for c_ in m_tab:
                c_.base += 16 * (CHUNKS * TURNS + 1)
            m_land.base += CREDIT - 1 + CHUNKS * TURNS
            for c_ in [m_bc, m_sel, m_tr, m_fin, m_ex, m_g, m_mg, m_out] + ([m_f1, m_h, m_f2, m_m, m_hi, m_r, m_mid, m_msg] if filtered else []):
                c_.base += CREDIT + CHUNKS * TURNS

        n_sems = {name: counter(f"node_{name}") for name in ("dve", "act", "pe", "pool")}
        n_part = [[counter(f"node_part_{k}_{b}") for k in range(TABLES)] for b in range(2)]
        n_store = counter("node_store")
        QUEUES = NT // NCH
        GROUPS = ((0, 8), (8, 16), (16, 20))

        def node_stage(n, last=False):
            ectx = ExitStack()
            with ectx:
                def sbn(name, shape, dt=F32):
                    return ectx.enter_context(nc.sbuf_tensor(f"{name}_n{n}", shape, dt))
                W = width[n - 1] if n else D
                parts = n in (2, 4)
                pin = [[sbn(f"pin{k}_{b}", [P, NCH, W]) for k in range(TABLES)] for b in range(2)] if parts else []
                ys = [sbn(f"y{q}", [P, NCH, D])[:, :, :] for q in range(QUEUES)]
                ts = [acc[:, q * NCH:(q + 1) * NCH, :] if parts else sbn(f"t{q}", [P, NCH, D])[:, :, :]
                      for q in range(QUEUES)]
                sts = [sbn(f"st{q}", [P, 6, NCH]) for q in range(QUEUES)]
                xTs = [sbn(f"xT{b}", [P, 4 * P]) for b in range(2)]
                hTs = [sbn(f"hT{b}", [P, 4 * P]) for b in range(2)]
                psT, psH, psO = psb[0:2], psb[2:4], psb[4:8]
                xv = xr[:, :].rearrange("p (t d) -> p t d", d=D)

                steps = []
                number = {k: c.base for k, c in n_sems.items()}

                def do(name, waits, make):
                    number[name] += 1
                    steps.append((name, [w for w in waits if w], make))
                    return (name, number[name])

                done = [None] * QUEUES

                def chain(q, name, make, extra=()):
                    done[q] = do(name, [done[q], *extra], make)
                    return done[q]

                def bcast(s, m=NCH):
                    return s.unsqueeze(2).to_broadcast([P, m, D])

                def rows(v, m=NCH):
                    return v.unsqueeze(1).to_broadcast([P, m, D])

                woven = []

                def weave():
                    for w in range(len(woven) + max(map(len, woven), default=0)):
                        for g in range(len(woven)):
                            if 0 <= w - g < len(woven[g]):
                                woven[g][w - g]()
                    woven.clear()

                def chained(q, *links):
                    woven.append([lambda name=name, make=make: chain(q, name, make) for name, make in links])

                def norm_first(q):
                    y, t, st = ys[q], ts[q], sts[q]
                    chained(q, ("dve", lambda e: e.tensor_reduce(st[:, 0, :], y, AX.X, ALU.add)),
                            ("dve", lambda e: e.tensor_scalar(st[:, 1, :], st[:, 0, :], 1.0 / D, None, ALU.mult)),
                            ("dve", lambda e: e.tensor_tensor(y, y, bcast(st[:, 1, :]), ALU.subtract)),
                            ("act", lambda e: e.activation(t, y, ACT.Square)))

                def norm_second(q, dst):
                    y, t, st = ys[q], ts[q], sts[q]
                    chained(q, ("dve", lambda e: e.tensor_reduce(st[:, 2, :], t, AX.X, ALU.add)),
                            ("dve", lambda e: e.tensor_scalar(st[:, 3, :], st[:, 2, :], 1.0 / D, EPS, ALU.mult, ALU.add)),
                            ("act", lambda e: e.activation(st[:, 2, :], st[:, 3, :], ACT.Sqrt)),
                            ("dve", lambda e: e.reciprocal(st[:, 3, :], st[:, 2, :])),
                            ("dve", lambda e: e.tensor_tensor(dst, y, bcast(st[:, 3, :]), ALU.mult)))

                count = [0]
                read = {}

                def transposed(src, m, after, b):
                    for k in range(0, m, 2):
                        p = do("pe", [after, read.get(("psT", b))],
                               lambda e, k=k: e.transpose(psT[b][:, k // 2 * P:(k // 2 + 1) * P],
                                                          src[:, k:k + 2, :].rearrange("p t d -> p (t d)"), ident[:, :]))
                    read["psT", b] = do("act", [p, read.get(("xT", b))],
                                        lambda e: e.activation(xTs[b][:, 0:m // 2 * P], psT[b][:, 0:m // 2 * P], ACT.Copy))
                    return read["psT", b]

                def product(xT, name, m, after, g, w, bias=None):
                    b, o = g % 2, g % 4
                    if bias is not None:
                        do("pe", [read.get(("psO", o))],
                           lambda e: e.matmul(psO[o][:, 0:m * D], onesb[0:PARTS, :],
                                              bias[:, :].unsqueeze(1).to_broadcast([PARTS, m, D]), start=True, stop=False))
                    for k in range(m // 2):
                        p = do("pe", [after, read.get(("psO", o))],
                               lambda e, k=k: e.matmul(psO[o][:, k * P:(k + 1) * P], xT[b][:, k * P:(k + 1) * P], w[:, :],
                                                       start=bias is None, stop=bias is None or k == m // 2 - 1))
                    read[name, b] = p
                    return p, psO[o][:, 0:m * D].rearrange("p (m d) -> p m d", d=D)

                part_read = {}

                def sums(q):
                    xq, y, st = xv[:, q * NCH:(q + 1) * NCH, :], ys[q], sts[q]
                    if parts:
                        p0, p1, p2, p3, p4 = (pin[q % 2][k][:, :, :] for k in range(TABLES))

                        def arrived(*k):
                            return [("part", i, q) for i in k]
                        other = do("pool", arrived(2, 3), lambda e: e.tensor_tensor(p2, p2, p3, ALU.add))
                        chain(q, "dve", lambda e: e.tensor_tensor(p0, p0, p1, ALU.add), arrived(0, 1))
                        chain(q, "dve", lambda e: e.tensor_tensor(p0, p0, p4, ALU.add), arrived(4))
                        chain(q, "dve", lambda e: e.tensor_tensor(p0, p0, p2, ALU.add), [other])
                        agg = p0[:, :, 0:D]
                    else:
                        agg = acc[:, q * NCH:(q + 1) * NCH, :]
                    dv = dinv[:, q * NCH:(q + 1) * NCH]
                    if n == 1:
                        chain(q, "dve", lambda e: e.scalar_tensor_tensor(out=y, in0=agg, scalar=0.0, in1=xq,
                                                                         op0=ALU.max, op1=ALU.add))
                    elif n == 4:
                        chain(q, "dve", lambda e: e.tensor_tensor(y, agg, bcast(dv), ALU.mult))
                        chain(q, "dve", lambda e: e.tensor_tensor(y, y, rows(bias3[:, :]), ALU.add))
                        chain(q, "dve", lambda e: e.tensor_tensor(y, y, xq, ALU.add))
                    else:
                        chain(q, "dve", lambda e: e.tensor_tensor(y, agg, xq, ALU.add))
                    if n == 2:
                        deg = p0[:, :, D]
                        chain(q, "dve", lambda e: e.tensor_scalar(st[:, 4, :], deg, 1.0, None, ALU.max))
                        sd = do("act", [done[q]], lambda e: e.activation(st[:, 5, :], st[:, 4, :], ACT.Sqrt))
                        chain(q, "dve", lambda e: e.reciprocal(st[:, 4, :], st[:, 5, :]), [sd])
                        chain(q, "dve", lambda e: e.tensor_scalar(st[:, 5, :], deg, 0.5, None, ALU.is_gt))
                        chain(q, "dve", lambda e: e.tensor_tensor(dv, st[:, 4, :], st[:, 5, :], ALU.mult))
                    part_read[q] = done[q]

                def affine(q):
                    xq, y = xv[:, q * NCH:(q + 1) * NCH, :], ys[q]
                    chained(q, ("pool", lambda e: e.tensor_tensor(y, y, rows(gamma[:, :]), ALU.mult)),
                            ("pool", lambda e: e.tensor_tensor(y, y, rows(beta[:, :]), ALU.add)),
                            ("dve", lambda e: e.tensor_tensor(y, y, xq, ALU.add)))

                def mlp(q):
                    for lo, hi in GROUPS:
                        woven.append(mlp_group(q, lo, hi, count[0], done[q]))
                        count[0] += 1

                def mlp_group(q, lo, hi, g, made):
                    m, b, y, v = hi - lo, g % 2, ys[q][:, lo:hi, :], {}

                    def turn():
                        v["ax"] = transposed(y, m, made, b)

                    def hidden():
                        p = do("pe", [v["ax"], read.get(("psH", b))],
                               lambda e: e.matmul(psH[b][:, 0:m // 2 * P], w1d[:, :], xTs[b][:, 0:m // 2 * P],
                                                  start=True, stop=True))
                        read["xT", b] = p
                        v["ah"] = do("act", [p, read.get(("hT", b))],
                                     lambda e: e.activation(hTs[b][:, 0:m // 2 * P], psH[b][:, 0:m // 2 * P], ACT.Relu,
                                                            bias=b1d[:, 0:1]))
                        read["psH", b] = v["ah"]

                    def result():
                        p, res = product(hTs, "hT", m, v["ah"], g, w2d, b2b)
                        x_ = xv[:, q * NCH + lo:q * NCH + hi, :]
                        read["psO", g % 4] = chain(q, "dve", lambda e: e.tensor_tensor(y, res, x_, ALU.add), [p])
                    return [turn, hidden, result]

                def dense(q):
                    for lo, hi in GROUPS:
                        woven.append(dense_group(q, lo, hi, count[0], done[q]))
                        count[0] += 1

                def dense_group(q, lo, hi, g, made):
                    m, b, v = hi - lo, g % 2, {}
                    cols_ = slice(q * NCH + lo, q * NCH + hi)
                    t, r, three = ts[q][:, lo:hi, :], ys[q][:, lo:hi, :], tab3[:, cols_, :, :]

                    def turn():
                        v["ax"] = transposed(xv[:, cols_, :], m, made, b)

                    def result():
                        v["p"], v["res"] = product(xTs, "xT", m, v["ax"], g, wld if n == 1 else w3d, blb if n == 1 else None)

                    def part0():
                        res = v["res"]
                        if n == 3:
                            v["p"] = do("dve", [v["p"]], lambda e: e.tensor_tensor(t, res, bcast(dinv[:, cols_], m), ALU.mult))
                            read["psO", g % 4] = v["p"]
                            v["res"] = t
                        res_ = v["res"]
                        v["a0"] = do("act", [v["p"]], lambda e: e.activation(three[:, :, 0, :], res_, ACT.Copy))

                    def part1():
                        res = v["res"]
                        d0 = do("dve", [v["p"], v["a0"]], lambda e: e.tensor_tensor(r, res, three[:, :, 0, :], ALU.subtract))
                        if n == 1:
                            read["psO", g % 4] = d0
                        v["a1"] = do("act", [d0], lambda e: e.activation(three[:, :, 1, :], r, ACT.Copy))

                    def part2():
                        done[q] = do("dve", [v["a1"]], lambda e: e.tensor_tensor(three[:, :, 2, :], r, three[:, :, 1, :],
                                                                                ALU.subtract))
                    return [turn, result, part0, part1, part2]

                def first(q):
                    for lo, hi in GROUPS:
                        woven.append(first_group(q, lo, hi, count[0]))
                        count[0] += 1

                def first_group(q, lo, hi, g):
                    m, v = hi - lo, {}

                    def turn():
                        v["ax"] = transposed(xv[:, q * NCH + lo:q * NCH + hi, :], m, None, g % 2)

                    def result():
                        p, res = product(xTs, "xT", m, v["ax"], g, w0d)
                        read["psO", g % 4] = done[q] = do("dve", [p], lambda e: e.tensor_copy(ys[q][:, lo:hi, :], res))
                    return [turn, result]

                def xq_of(q):
                    return xv[:, q * NCH:(q + 1) * NCH, :]
                sections = {
                    0: [first],
                    1: [sums, norm_first, lambda q: norm_second(q, xq_of(q)), dense],
                    2: [sums, norm_first, lambda q: norm_second(q, ys[q]), affine, norm_first,
                        lambda q: norm_second(q, xq_of(q))],
                    3: [sums, mlp, norm_first, lambda q: norm_second(q, xq_of(q)), dense],
                    4: [sums, norm_first, lambda q: norm_second(q, xq_of(q))],
                }[n]
                for wave in range(QUEUES + len(sections) - 1):
                    for s in range(len(sections) - 1, -1, -1):
                        if 0 <= wave - s < QUEUES:
                            sections[s](wave - s)
                    if n or wave == QUEUES - 1:
                        weave()

                def run(name, eng):
                    own = n_sems[name]
                    for who, waits, make in steps:
                        if who != name:
                            continue
                        for w in waits:
                            if w[0] == "part":
                                c_ = n_part[w[2] % 2][w[1]]
                                eng.wait_ge(c_.sem, c_.at(16 * (w[2] // 2 + 1)))
                            else:
                                eng.wait_ge(n_sems[w[0]].sem, w[1])
                        make(eng).then_inc(own.sem, 1)

                with nc.Block() as block:
                    @block.sync
                    def _(sp):
                        for q in range(QUEUES if parts else 0):
                            if q >= 2:
                                sp.wait_ge(n_sems["dve"].sem, part_read[q - 2][1])
                            for k in range(TABLES):
                                sp.dma_start(pin[q % 2][k][:, :, :].rearrange("p a w -> p (a w)"),
                                             part[n - 1][k][0:ROWS, :].rearrange("(p a) w -> p (a w)", p=P)
                                             [:, q * NCH * W:(q + 1) * NCH * W]).then_inc(n_part[q % 2][k].sem, 16)
                        if n in (0, 2, 4):
                            dst = out if last else table[n].rearrange("(p t) d -> p (t d)", p=P)
                            for q in range(QUEUES):
                                sp.wait_ge(n_sems["dve"].sem, done[q][1])
                                at = slice(q * NCH * D, (q + 1) * NCH * D)
                                rows_ = xr[:, at] if n else ys[q].rearrange("p t d -> p (t d)")
                                sp.dma_start(dst[:, at], rows_).then_inc(n_store.sem, 16)
                            sp.wait_ge(n_store.sem, n_store.at(16 * QUEUES))

                    @block.vector
                    def _(eng):
                        run("dve", eng)

                    @block.scalar
                    def _(eng):
                        run("act", eng)

                    @block.tensor
                    def _(eng):
                        run("pe", eng)

                    @block.gpsimd
                    def _(eng):
                        run("pool", eng)
                for k_, c_ in n_sems.items():
                    c_.base = number[k_]
                if parts:
                    for b in range(2):
                        for c_ in n_part[b]:
                            c_.base += 16 * len(range(b, QUEUES, 2))
                if n in (0, 2, 4):
                    n_store.base += 16 * QUEUES

        node_stage(0)
        near_sum_pass(0, ew_d=a["ewT"])
        far_pass(0, 0, 1, ew_d=a["ewT"])
        far_collect(0)
        node_stage(1)
        near_read_pass(1, filtered=True)
        far_pass(1, 1, 0, filtered=True)
        node_stage(2)
        near_sum_pass(2)
        far_pass(2, 0, 1)
        far_collect(2)
        node_stage(3)
        near_read_pass(3)
        far_pass(3, 1, 0)
        node_stage(4, last=True)


def kernel(**inputs):
    import numpy as _np
    import concourse.bacc as _bacc
    from concourse import mybir as _mybir
    from concourse.bass_utils import run_bass_kernel_spmd as _run

    nc = _bacc.Bacc("TRN2", target_bir_lowering=False, num_devices=1)
    i = {k: _np.asarray(v) for k, v in inputs.items()}
    ea = i["edge_attr_64"].reshape(TILES // CHUNK, CHUNK, P, D)
    laid = {
        "x": _np.pad(i["x"], ((0, ROWS - NODES), (0, 0))).reshape(NT, P, D).transpose(1, 0, 2).reshape(P, NT * D),
        "srcT": i["src"].reshape(TILES, P).T,
        "dstT": i["dst"].reshape(TILES, P).T,
        "ewT": i["edge_weight"].reshape(TILES, P).T,
        "src": i["src"].reshape(TURNS, GROUP * P), "dst": i["dst"].reshape(TURNS, GROUP * P),
        "ea2": ea[:, :CHUNK // 2 * 2].reshape(-1, CHUNK // 2, 2, P, D).transpose(2, 4, 0, 1, 3).reshape(P, -1),
        "ea1": ea[:, CHUNK - 1].transpose(2, 0, 1).reshape(D, -1),
        "L0_gnn_W": i["L0_gnn_W"],
        "WlT": i["L1_gnn_Wl"].T, "bl": i["L1_gnn_bl"].reshape(1, D),
        "Wf1T": i["L1_gnn_Wf1"].T, "bf1": i["L1_gnn_bf1"].reshape(D, 1),
        "Wf2T": i["L1_gnn_Wf2"].T, "bf2": i["L1_gnn_bf2"].reshape(1, D),
        "L2_gnn_W1": i["L2_gnn_W1"], "b1": i["L2_gnn_b1"].reshape(D, 1),
        "L2_gnn_W2": i["L2_gnn_W2"], "b2": i["L2_gnn_b2"].reshape(1, D),
        "L3_gnn_weight": i["L3_gnn_weight"],
        "gamma": i["L1_gnn_gamma"].reshape(1, D), "beta": i["L1_gnn_beta"].reshape(1, D),
        "bias3": i["L3_gnn_bias"].reshape(1, D),
    }
    arrays, args = {}, {}
    for name, v in laid.items():
        v = _np.ascontiguousarray(v)
        arrays[f"in_{name}"] = v
        args[name] = nc.dram_tensor(f"in_{name}", v.shape, _mybir.dt.from_np(v.dtype), kind="ExternalInput").ap()
    out = nc.dram_tensor("out_rows", (P, NT * D), _mybir.dt.float32, kind="ExternalOutput").ap()
    build(nc, args, out)
    r = _run(nc, [arrays], core_ids=[0])
    return r.results[0]["out_rows"].reshape(P, NT, D).transpose(1, 0, 2).reshape(ROWS, D)[:NODES]
```
